# Optimizing a Trainium2 kernel written in Bass

```python
import numpy as np
import jax
import jax.numpy as jnp

def _softmax(x, axis=-1):
    return jax.nn.softmax(x, axis=axis)

def _gelu(x):
    return jax.nn.gelu(x, approximate=True)

def _silu(x):
    return jax.nn.silu(x)

def _sigmoid(x):
    return jax.nn.sigmoid(x)

def _layernorm(x, axis=-1, eps=1e-05):
    m = jnp.mean(x, axis=axis, keepdims=True)
    v = jnp.var(x, axis=axis, keepdims=True)
    return (x - m) / jnp.sqrt(v + eps)

def _scatter_add(tgt, idx, src, axis=0):
    return tgt.at[idx].add(src)

def _segment_sum(src, seg, n):
    return jax.ops.segment_sum(src, seg, n)
kernel_name = 'mk_seq_preln_d1_jaxref_r8_fcc31f'

def setup_inputs(seed: int=0):
    np.random.seed(seed)
    _w = jnp.asarray

    def _L0_attn_setup():
        import jax, jax.numpy as jnp
        import numpy as np
        B, T, C = (64, 32, 128)
        N_HEAD, HEAD_SIZE, KV_RANK = (16, 64, 128)
        BLOCK_SIZE = 32
        key = jax.random.key(seed)
        ks = jax.random.split(key, 5)
        HD = N_HEAD * HEAD_SIZE

        def init(k, shape):
            fan_in = shape[0]
            bound = 1.0 / np.sqrt(fan_in)
            return jax.random.uniform(k, shape, jnp.float32, -bound, bound)
        return {'x': jax.random.normal(ks[0], (B, T, C), jnp.float32), 'w_kv_down': init(ks[1], (C, KV_RANK)), 'w_kv_up': init(ks[2], (KV_RANK, 2 * HD)), 'w_q': init(ks[3], (C, HD)), 'w_out': init(ks[4], (HD, C))}
    _L0_attn_in = _L0_attn_setup()

    def _L0_ffn_setup():
        import jax, jax.numpy as jnp
        import numpy as np
        D_MODEL = 128
        HIDDEN = 512
        NUM_EXPERTS = 8
        TOP_K = 2
        DEPTH = 12
        DEPTH_SCALE = 1.0 / np.sqrt(DEPTH)
        key = jax.random.key(seed)
        k_x, k_r, k_g, k_u, k_d = jax.random.split(key, 5)
        s_in = 1.0 / np.sqrt(D_MODEL)
        s_hid = 1.0 / np.sqrt(HIDDEN)
        return {'x': jax.random.normal(k_x, (2, 256, D_MODEL), dtype=jnp.float32), 'Wr': jax.random.normal(k_r, (D_MODEL, NUM_EXPERTS), dtype=jnp.float32) * s_in, 'Wg': jax.random.normal(k_g, (NUM_EXPERTS, D_MODEL, HIDDEN), dtype=jnp.float32) * s_in, 'Wu': jax.random.normal(k_u, (NUM_EXPERTS, D_MODEL, HIDDEN), dtype=jnp.float32) * s_in, 'Wd': jax.random.normal(k_d, (NUM_EXPERTS, HIDDEN, D_MODEL), dtype=jnp.float32) * s_hid}
    _L0_ffn_in = _L0_ffn_setup()
    _d = {'L0_attn_x': _L0_attn_in['x'], 'L0_attn_w_kv_down': _L0_attn_in['w_kv_down'], 'L0_attn_w_kv_up': _L0_attn_in['w_kv_up'], 'L0_attn_w_q': _L0_attn_in['w_q'], 'L0_attn_w_out': _L0_attn_in['w_out'], 'L0_ffn_Wr': _L0_ffn_in['Wr'], 'L0_ffn_Wg': _L0_ffn_in['Wg'], 'L0_ffn_Wu': _L0_ffn_in['Wu'], 'L0_ffn_Wd': _L0_ffn_in['Wd']}
    _x0 = _d['L0_attn_x']
    _d['L0_attn_x'] = jax.random.normal(jax.random.fold_in(jax.random.key(seed), 1), (8, 512, 128), dtype=_x0.dtype)
    del _x0
    return _d

def reference(L0_attn_x, L0_attn_w_kv_down, L0_attn_w_kv_up, L0_attn_w_q, L0_attn_w_out, L0_ffn_Wr, L0_ffn_Wg, L0_ffn_Wu, L0_ffn_Wd):

    def _L0_attn_ref(x, w_kv_down, w_kv_up, w_q, w_out):
        import jax, jax.numpy as jnp
        import numpy as np
        B, T, C = (64, 32, 128)
        N_HEAD, HEAD_SIZE, KV_RANK = (16, 64, 128)
        BLOCK_SIZE = 32
        Bx, Tx, Cx = x.shape
        HD = N_HEAD * HEAD_SIZE
        latent_kv = x @ w_kv_down
        kv = latent_kv @ w_kv_up
        k, v = (kv[..., :HD], kv[..., HD:])
        k = k.reshape(Bx, Tx, N_HEAD, HEAD_SIZE)
        v = v.reshape(Bx, Tx, N_HEAD, HEAD_SIZE)
        q = (x @ w_q).reshape(Bx, Tx, N_HEAD, HEAD_SIZE)
        scale = HEAD_SIZE ** (-0.5)
        att = jnp.einsum('bqhd,bkhd->bhqk', q, k) * scale
        causal = jnp.tril(jnp.ones((Tx, Tx), dtype=bool))
        att = jnp.where(causal, att, -jnp.inf)
        att = jax.nn.softmax(att, axis=-1)
        y = jnp.einsum('bhqk,bkhd->bqhd', att, v)
        y = y.reshape(Bx, Tx, HD)
        return y @ w_out

    def _L0_ffn_ref(x, Wr, Wg, Wu, Wd):
        import jax, jax.numpy as jnp
        import numpy as np
        D_MODEL = 128
        HIDDEN = 512
        NUM_EXPERTS = 8
        TOP_K = 2
        DEPTH = 12
        DEPTH_SCALE = 1.0 / np.sqrt(DEPTH)
        B, T, C = x.shape
        flat_x = x.reshape(-1, C)
        logits = flat_x @ Wr
        top_vals, top_idx = jax.lax.top_k(logits, TOP_K)
        rw = jax.nn.softmax(top_vals.astype(jnp.float32), axis=-1).astype(x.dtype)
        combine = jnp.sum(rw[..., None] * jax.nn.one_hot(top_idx, NUM_EXPERTS, dtype=x.dtype), axis=1)
        g = jnp.einsum('nc,ech->neh', flat_x, Wg)
        u = jnp.einsum('nc,ech->neh', flat_x, Wu)
        h = jax.nn.silu(g) * u
        eo = jnp.einsum('neh,ehc->nec', h, Wd) * DEPTH_SCALE
        out = jnp.einsum('ne,nec->nc', combine, eo)
        return out.reshape(B, T, C)
    x = L0_attn_x
    x = x + _L0_attn_ref(_layernorm(x, axis=-1), L0_attn_w_kv_down, L0_attn_w_kv_up, L0_attn_w_q, L0_attn_w_out)
    x = x + _L0_ffn_ref(_layernorm(x, axis=-1), L0_ffn_Wr, L0_ffn_Wg, L0_ffn_Wu, L0_ffn_Wd)
    return x

_drawn_inputs = setup_inputs


def setup_inputs(seed=0):
    import zlib

    import numpy as np

    out = dict(_drawn_inputs(seed))
    spreads = {}
    factors = {'L0_attn_w_q': 6.597}
    for name, (base, spread) in spreads.items():
        noise = np.random.default_rng([zlib.crc32(name.encode()), seed]).standard_normal(out[name].shape)
        drawn = base * np.exp(spread * noise) if base else spread * noise
        out[name] = jnp.asarray(drawn.astype(out[name].dtype))
    for name, factor in factors.items():
        out[name] = (out[name] * factor).astype(out[name].dtype)
    return out
```

```python
from contextlib import ExitStack

import numpy as np
import concourse.bass as bass
from concourse import mybir

F32 = mybir.dt.float32
F32R = mybir.dt.float32r
BF16 = mybir.dt.bfloat16
I32 = mybir.dt.int32
U32 = mybir.dt.uint32
ALU = mybir.AluOpType
ACT = mybir.ActivationFunctionType
AX = mybir.AxisListType

P = 128
B, T, C = 8, 512, 128
NT = T // P
NH, HD = 16, 64
NP = NH // 2
R = 128
NTOK = B * T
TILES = NTOK // P
RING = 4
E, HID, K = 8, 512, 2
HC = HID // P
STEPS = B * NP
REGION = NTOK
ROW = C + 2
SLOTS = (NTOK * K + E * (P - 1)) // P
TURNS, LEFT = divmod(SLOTS, RING)
SCALE = HD ** -0.5
DEPTH_SCALE = 12 ** -0.5
EPS = 1e-5
MASKED = -1e30
BIG = 3e38
RANK_COL, TOTAL_COL = 64, 128


def seen(eng, sem, count):
    if not isinstance(count, int) or count > 0:
        eng.wait_ge(sem, count)


def before(m, q):
    return (m, q - 1) if q else (m - 1, RING - 1)


def after(m, q):
    return (m, q + 1) if q < RING - 1 else (m + 1, 0)


def layer(nc, x, w_down, w_up, w_q, w_out, Wr, Wg, Wu, Wd, out):
    ctx = ExitStack()
    with ctx:
        def sb(name, shape, dt=F32):
            return ctx.enter_context(nc.sbuf_tensor(name, shape, dt))

        def sem(name):
            return ctx.enter_context(nc.semaphore(name))

        xn_dram = nc.dram_tensor("xn_scratch", [B, P, 2 * T], F32).ap()
        rows_dram = nc.dram_tensor("routed_rows", [E * REGION, ROW], F32).ap()
        expert_dram = nc.dram_tensor("expert_out", [K * NTOK, C], F32).ap()

        X = sb("X", [P, TILES, C])
        XT = sb("XT", [P, 2, NTOK], F32R)
        GU = sb("GU", [P, NP, 1024], F32R)
        W_ffn = sb("W_ffn", [P, E, 2 * HID])
        W_dn = sb("W_dn", [P, E, HC, C])
        prob = sb("prob", [P, 2 * 1280])
        PT = sb("PT", [P, 2, 3072], F32R)
        t_sb = sb("t_sb", [P, 2, 2, T], F32R)
        y_sb = sb("y_sb", [P, 2, 2, T], F32R)
        G_cur = sb("G_cur", [P, 2, 2, P], F32R)
        U_cur = sb("U_cur", [P, 2, 2, P], F32R)
        xn_cur = sb("xn_cur", [P, 2, NT, C], F32R)
        mask = sb("mask", [P, T])
        ident = sb("ident", [P, P])
        zero_bf = sb("zero_bf", [P, T], BF16)
        wdT = sb("wdT", [P, P])
        wqT = sb("wqT", [P, P])
        wkT = sb("wkT", [P, P])
        wvT = sb("wvT", [P, P])
        row_sum = sb("row_sum", [P, NT, 2])
        row_inv = sb("row_inv", [P, NT, 2])
        neg_max = sb("neg_max", [P, NT, 2])
        stats = sb("stats", [P, TILES, 6])
        mv = sb("mv", [P, TILES, 2])
        rstd = sb("rstd", [P, TILES])
        power = sb("power", [P, TILES])
        eps = sb("eps", [P, NT])
        outT = sb("outT", [P, T])
        Wr_sb = sb("Wr_sb", [P, E])
        routed = sb("routed", [P, K, NT, ROW])
        xn2T = sb("xn2T", [P, T])
        before_bf = sb("before_bf", [P, P], BF16)
        ones_bf = sb("ones_bf", [P, P], BF16)
        const_i = sb("const_i", [P, P], I32)
        expert_id = sb("expert_id", [P, NT, E])
        slot_id = sb("slot_id", [P, SLOTS])
        dest = sb("dest", [P, K, NT])
        logit = sb("logit", [P, NT, E])
        top = sb("top", [P, NT, 8])
        top_i = sb("top_i", [P, NT, 8], U32)
        top_f = sb("top_f", [P, NT, K])
        chosen = sb("chosen", [P, K, NT, E])
        chosen_bf = sb("chosen_bf", [P, NT, E], BF16)
        gap = sb("gap", [P, NT])
        gap_exp = sb("gap_exp", [P, NT])
        weight = sb("weight", [P, K, NT])
        base = sb("base", [P, E])
        pos = sb("pos", [P, NT, E])
        picked = sb("picked", [P, K, NT, E])
        row_f = sb("row_f", [P, K, NT])
        row_i = sb("row_i", [P, K, NT], I32)
        count = sb("count", [1, E])
        count_i = sb("count_i", [1, E], I32)
        tiles_of = sb("tiles_of", [1, E])
        ends = sb("ends", [1, E])
        jump = sb("jump", [1, E])
        past, jumps = (prob[0:1, o:o + SLOTS * (E - 1)].rearrange("p (j e) -> p j e", e=E - 1) for o in (0, T))
        table_f = sb("table_f", [1, 2, SLOTS])
        table = sb("table", [1, 2, SLOTS], I32)
        gate_v = sb("gate_v", [P, 1], I32)
        gate_p = sb("gate_p", [P, RING + 1])
        meta_w = sb("meta_w", [P, RING])
        meta_row = sb("meta_row", [P, RING], I32)
        up_hi = GU[:, :, :]
        up_lo = XT[:, :, :].rearrange("p a n -> p (a n)").rearrange("p (e n) -> p e n", e=E)
        x_in_tile = [routed[:, 0, q, :] for q in range(RING)]
        xT_tile = [t_sb[:, q, :, 0:P] for q in range(2)]
        silu_sb = [prob[:, q * T:(q + 1) * T] for q in range(2)]
        h_sb = [prob[:, (2 + q) * T:(3 + q) * T] for q in range(2)]
        hT_sb = [outT, xn2T]
        eo_sb = [prob[:, 4 * T + q * C:4 * T + (q + 1) * C] for q in range(2)]
        back = W_ffn[:, :, :].rearrange("p e n -> p (e n)").rearrange("p (k t c) -> p k t c", k=K, c=C)

        w_up_sb = W_ffn[:, 0:2, :].rearrange("p a n -> p (a n)")
        w_q_sb = W_ffn[:, 2, :]
        w_out_sb = W_ffn[:, 3, :].rearrange("p (g c) -> p g c", g=NP)
        w_down_sb = W_ffn[:, 4, 0:R]
        xn_f32 = prob[:, 0:2 * T].rearrange("p (q t c) -> p q t c", q=2, c=C)

        s_ps = [ctx.enter_context(nc.psum_tensor(f"s_ps{h}", [P, T], F32)) for h in range(2)]
        pt_ps = ctx.enter_context(nc.psum_tensor("pt_ps", [P, 2, NT, P], F32))
        t_ps = ctx.enter_context(nc.psum_tensor("t_ps", [P, T], F32))
        y_ps = ctx.enter_context(nc.psum_tensor("y_ps", [P, 2, 256], F32))
        out_ps = ctx.enter_context(nc.psum_tensor("out_ps", [P, T], F32))
        post_ps = ctx.enter_context(nc.psum_tensor("post_ps", [P, T], F32))

        gu_ps = [ps[:, 0:256].rearrange("p (k c) -> p k c", k=2) for ps in (s_ps[1], t_ps)]

        g_ps = [s_ps[0][:, :], t_ps[:, :]]
        u_ps = [s_ps[1][:, :], y_ps[:, :, :].rearrange("p h q -> p (h q)")]
        eo_ps = [pt_ps[:, q, 0, :] for q in range(2)]

        def gu_at(g, part, h):
            return GU[:, g, :].rearrange("p (k a h c) -> p k a h c", k=2, a=2, h=2)[:, :, part, h, :]

        def p_pair(i):
            o = P * i * (i + 1)
            return prob[:, o:o + 2 * P * (i + 1)].rearrange("p (h k) -> p h k", h=2)

        def p_at(i, h):
            o = 128 * i * (i + 1) + h * 128 * (i + 1)
            return prob[:, o:o + 128 * (i + 1)]

        def pt_at(part, half):
            v = PT[:, part, 0:1024] if half == 0 else PT[:, part, 1024:3072]
            return v.rearrange("p (j h i q) -> p j h i q", h=2, i=2, q=P)

        x_in = [sem(f"x_in{k}") for k in range(4)]
        w_in = sem("w_in")
        consts = sem("consts")
        S = {n: sem(n) for n in (
            "stats_done", "aggr_done", "rstd_done", "xn_done", "xnhi_done", "xnlo_done", "xn_stored0", "xn_stored1", "xT_ready", "xThi_done", "xTlo_done",
            "wdT_ready", "wdT_copied", "wqT_ready", "wkT_ready", "wvT_ready", "wT_copied", "gu_ready", "guhi_done", "gulo_done",
            "g_loaded", "u_loaded", "xn_loaded",
            "t_ready", "thi_done", "tlo_done", "s_ready", "max_done", "exp_done", "inv_done", "norm_dve", "norm_pool",
            "pt_ready", "pthi_done", "ptlo_done", "y_ready", "yhi_done", "ylo_done", "out_ready",
            "outT_copied", "outT_ready", "x2_done", "stats2", "rstd2", "xn2_done", "xn2T_ready", "xn2T_copied", "rows_copied",
            "logits_ready", "routing", "chosen_done", "gap_done", "gap_exp_done", "ranks_ready", "rows_done", "rows_written", "dest_done", "base_set", "gated",
            "wr_in", "zero_tile", "ffn_up_in", "ffn_down_in", "table_done", "tabling", "up_hi_done", "up_lo_done",
            "x_tile_in0", "x_tile_in1", "x_tile_in2", "x_tile_in3", "x_tile_T", "x_hi", "x_lo", "meta_done", "g_ready", "u_ready", "silu_done", "h_done",
            "hT_ready", "hT_copied", "eo_ready", "eo_done", "eo_out0", "eo_out1", "eo_out2", "eo_out3", "added", "stored")}
        back_in = [sem(f"back_in{k}") for k in range(4)]

        block = ctx.enter_context(nc.Block())
        SPLIT = 2

        @block.sync
        def _(sp):
            sp.dma_start(w_down_sb, w_down).then_inc(w_in, 16)
            sp.dma_start(w_up_sb, w_up).then_inc(w_in, 16)
            sp.dma_start(w_q_sb, w_q).then_inc(w_in, 16)
            sp.dma_start(w_out_sb, w_out.rearrange("(g d) c -> d g c", d=P)).then_inc(w_in, 16)
            for k in range(4):
                n = TILES // 4
                sp.dma_start(X[:, k * n:(k + 1) * n, :],
                             x[k * n * P:(k + 1) * n * P, :].rearrange("(t p) c -> p t c", p=P)).then_inc(x_in[k], 16)
            sp.dma_start(Wr_sb[:, :], Wr).then_inc(S["wr_in"], 16)
            def store_xn(m):
                for q in range(SPLIT):
                    b = m * SPLIT + q
                    seen(sp, S["xnlo_done"], b + 1)
                    sp.dma_start(xn_dram[bass.ds(b, 1), :, :].rearrange("b p (a n) -> p (b a) n", a=2),
                                 PT[:, :, q * T:(q + 1) * T].bitcast(F32)).then_inc(S[f"xn_stored{q}"], 16)

            store_xn(0)
            with sp.Fori(1, B // SPLIT) as m:
                store_xn(m)

            sp.wait_ge(S["gulo_done"], NP)
            sp.wait_ge(S["xn_stored0"], 16 * B // 2)
            sp.wait_ge(S["xn_stored1"], 16 * B // 2)

            def load_g(n):
                seen(sp, S["t_ready"], 2 * n + 2)
                p = (n + 1) % NP
                sp.dma_start(G_cur[:, :, :, :].rearrange("p a h c -> p (a h c)").bitcast(F32),
                             GU[:, bass.ds(p, 1), 0:512].rearrange("p a n -> p (a n)").bitcast(F32)).then_inc(S["g_loaded"], 16)

            def load_u(n):
                seen(sp, S["out_ready"], 2 * n + 2)
                p = (n + 1) % NP
                sp.dma_start(U_cur[:, :, :, :].rearrange("p a h c -> p (a h c)").bitcast(F32),
                             GU[:, bass.ds(p, 1), 512:1024].rearrange("p a n -> p (a n)").bitcast(F32)).then_inc(S["u_loaded"], 16)

            def load_xn(b):
                seen(sp, S["y_ready"], 2 * NP * b)
                sp.dma_start(xn_cur[:, :, :, :].rearrange("p a t c -> p (a t c)").bitcast(F32),
                             xn_dram[bass.ds(b, 1), :, :].rearrange("b p n -> p (b n)")).then_inc(S["xn_loaded"], 16)

            sp.dma_start(W_ffn[:, :, 0:HID], Wg.rearrange("e c n -> c e n")).then_inc(S["ffn_up_in"], 16)
            sp.dma_start(W_ffn[:, :, HID:2 * HID], Wu.rearrange("e c n -> c e n")).then_inc(S["ffn_up_in"], 16)
            load_g(-1)
            load_u(-1)
            load_xn(0)
            load_g(0)
            load_g(1)
            sp.wait_ge(S["rows_written"], 16)
            sp.dma_start(W_dn[:, :, :, :], Wd.rearrange("e (h p) c -> p e h c", p=P)).then_inc(S["ffn_down_in"], 16)
            with sp.Fori(2, STEPS - 1) as n:
                load_g(n)
                with sp.If((n % NP) == 1):
                    load_xn(n // NP)
                load_u(n - 2)
            load_u(STEPS - 3)
            load_u(STEPS - 2)

            sp.wait_ge(S["table_done"], 1)
            sp.wait_ge(S["rows_written"], 16 * (K * NT * B + 1))

            def load_tile(m, q):
                j = RING * m + q
                row = nc.sync.value_load(table[0:1, 1, bass.ds(j, 1)], min_val=0, max_val=E * REGION - P)
                src = rows_dram[bass.ds(nc.sync.snap(row), P), :]
                seen(sp, S["meta_done"], 2 * (j - RING + 1))
                sp.dma_start(x_in_tile[q], src).then_inc(S[f"x_tile_in{q}"], 16)

            for q in range(RING):
                load_tile(0, q)
            with sp.Fori(1, TURNS) as m:
                for q in range(RING):
                    load_tile(m, q)
            for q in range(LEFT):
                load_tile(TURNS, q)
            for q in range(RING):
                sp.wait_ge(S[f"eo_out{q}"], 16 * (TURNS + (q < LEFT)))
            n = TILES // 4
            for k in range(4):
                for a in range(K):
                    r = a * NTOK + k * n * P
                    sp.dma_start(back[:, a, k * n:(k + 1) * n, :],
                                 expert_dram[r:r + n * P, :].rearrange("(t p) c -> p t c", p=P)).then_inc(back_in[k], 16)
            for k in range(4):
                sp.wait_ge(S["added"], 2 * k + 2)
                sp.dma_start(out[k * n * P:(k + 1) * n * P, :].rearrange("(t p) c -> p t c", p=P),
                             X[:, k * n:(k + 1) * n, :]).then_inc(S["stored"], 16)
            sp.wait_ge(S["stored"], 64)

        @block.gpsimd
        def _(pool):
            nc.gpsimd.memset(ident[:, :], 0.0).then_inc(consts, 1)
            nc.gpsimd.memset(mask[:, :], 0.0).then_inc(consts, 1)
            nc.gpsimd.memset(zero_bf[:, :], 0.0).then_inc(consts, 1)
            nc.gpsimd.memset(power[:, :], -0.5).then_inc(consts, 1)
            nc.gpsimd.memset(eps[:, :], EPS)
            nc.gpsimd.memset(W_dn[:, :, :, :].rearrange("p e h c -> p (e h c)")[:, 0:8 * ROW], 0.0).then_inc(S["zero_tile"], 1)
            pool.wait_ge(consts, 2)
            nc.gpsimd.affine_select(out=ident[:, :], in_=ident[:, :], compare_op=ALU.not_equal, fill=1.0,
                                    base=0, pattern=[[-1, P]], channel_multiplier=1).then_inc(consts, 1)
            nc.gpsimd.affine_select(out=mask[:, T - P:T], in_=mask[:, T - P:T], compare_op=ALU.is_ge, fill=MASKED,
                                    base=0, pattern=[[-1, P]], channel_multiplier=1).then_inc(consts, 1)
            pool.wait_ge(S["zero_tile"], 1)
            n = E * REGION * ROW // P // (8 * ROW)
            nc.gpsimd.dma_start(rows_dram.rearrange("(p a r) c -> p a (r c)", p=P, a=n),
                         W_dn[:, :, :, :].rearrange("p e h c -> p (e h c)")[:, 0:8 * ROW].unsqueeze(1).to_broadcast([P, n, 8 * ROW])
                         ).then_inc(S["rows_written"], 16)
            nc.gpsimd.memset(before_bf[:, :], 0.0).then_inc(consts, 1)
            nc.gpsimd.memset(ones_bf[:, :], 1.0).then_inc(consts, 1)
            pool.wait_ge(consts, 8)
            nc.gpsimd.affine_select(out=before_bf[:, :], in_=before_bf[:, :], compare_op=ALU.is_ge, fill=1.0,
                                    base=0, pattern=[[-1, P]], channel_multiplier=1).then_inc(consts, 1)
            nc.gpsimd.iota(const_i[:, 0:NT * E], pattern=[[0, NT], [1, E]], base=0, channel_multiplier=0).then_inc(consts, 1)
            pool.wait_ge(consts, 10)
            nc.gpsimd.tensor_copy(expert_id[:, :, :].rearrange("p t e -> p (t e)"), const_i[:, 0:NT * E]).then_inc(consts, 1)
            pool.wait_ge(consts, 11)
            nc.gpsimd.iota(const_i[:, 0:SLOTS], pattern=[[1, SLOTS]], base=0, channel_multiplier=0).then_inc(consts, 1)
            pool.wait_ge(consts, 12)
            nc.gpsimd.tensor_copy(slot_id[:, :], const_i[:, 0:SLOTS]).then_inc(consts, 1)
            pool.wait_ge(consts, 13)
            nc.gpsimd.iota(const_i[:, 0:K * NT], pattern=[[NTOK, K], [P, NT]], base=1 - T, channel_multiplier=1).then_inc(consts, 1)
            pool.wait_ge(consts, 14)
            nc.gpsimd.tensor_copy(dest[:, :, :].rearrange("p k t -> p (k t)"), const_i[:, 0:K * NT]).then_inc(consts, 1)
            pool.wait_ge(S["aggr_done"], TILES)
            pool.wait_ge(consts, 6)
            nc.gpsimd.tensor_scalar(rstd[:, :], mv[:, :, 1], EPS, None, ALU.add).then_inc(S["rstd_done"], 1)
            pool.wait_ge(S["rstd_done"], 1)
            nc.gpsimd.tensor_tensor(rstd[:, :], rstd[:, :], power[:, :], ALU.pow).then_inc(S["rstd_done"], 1)

            def norm(n, i):
                seen(pool, S["inv_done"], NT * n + i + 1)
                nc.gpsimd.tensor_tensor(p_pair(i), p_pair(i),
                                        row_inv[:, i, :].unsqueeze(2).to_broadcast([P, 2, P * (i + 1)]),
                                        ALU.mult).then_inc(S["norm_pool"], 1)

            def post_rstd(b):
                seen(pool, S["stats2"], 8 * b + 8)
                nc.gpsimd.tensor_tensor(rstd[:, 0:NT], mv[:, 0:NT, 1], eps[:, :], ALU.add).then_inc(S["rstd2"], 1)
                seen(pool, S["rstd2"], 2 * b + 1)
                nc.gpsimd.tensor_tensor(rstd[:, 0:NT], rstd[:, 0:NT], power[:, 0:NT], ALU.pow).then_inc(S["rstd2"], 1)

            def post_scatter(b):
                seen(pool, S["rows_done"], b + 1)
                nc.gpsimd.tensor_tensor(gate_p[:, RING:RING + 1], eps[:, 0:1], eps[:, 0:1], ALU.add)
                for k in range(K):
                    for t in range(NT):
                        nc.gpsimd.indirect_dma_start(
                            out=rows_dram, out_offset=bass.IndirectOffsetOnAxis(ap=row_i[:, k, t:t + 1], axis=0),
                            in_=routed[:, k, t, :], in_offset=None).then_inc(S["rows_written"], 16)

            pool.wait_ge(S["rows_written"], 16)
            norm(0, 2)
            with pool.Fori(1, 9) as n:
                norm(n - 1, 3)
                norm(n, 2)
            with pool.Fori(1, STEPS - 1 - NP) as v:
                norm(v + NP - 1, 3)
                norm(v + NP, 2)
                with pool.If((v % NP) == 2):
                    post_rstd(v // NP)
                with pool.If((v % NP) == 6):
                    post_scatter(v // NP)
            norm(STEPS - 2, 3)
            norm(STEPS - 1, 2)
            norm(STEPS - 1, 3)
            post_rstd(B - 1)
            post_scatter(B - 1)

            def scatter_tile(m, q):
                j = RING * m + q
                seen(pool, S["eo_done"], j + 1)
                nc.gpsimd.tensor_tensor(gate_p[:, q:q + 1], eps[:, 0:1], eps[:, 0:1], ALU.add)\
                    .then_inc(S["gated"], 1)
                nc.gpsimd.indirect_dma_start(
                    out=expert_dram, out_offset=bass.IndirectOffsetOnAxis(ap=meta_row[:, q:q + 1], axis=0),
                    in_=eo_sb[q % 2], in_offset=None, bounds_check=K * NTOK - 1, oob_is_err=False).then_inc(S[f"eo_out{q}"], 16)

            for q in range(RING):
                scatter_tile(0, q)
            with pool.Fori(1, TURNS) as m:
                for q in range(RING):
                    scatter_tile(m, q)
            for q in range(LEFT):
                scatter_tile(TURNS, q)

        @block.scalar
        def _(act):
            act.wait_ge(S["wdT_ready"], 1)
            nc.scalar.activation(wdT[:, :], post_ps[:, 0:P], ACT.Copy).then_inc(S["wdT_copied"], 1)
            for g in range(NP):
                act.wait_ge(S["wqT_ready"], g + 1)
                if g:
                    act.wait_ge(S["gu_ready"], g)
                nc.scalar.activation(wqT[:, :], s_ps[0][:, 0:P], ACT.Copy).then_inc(S["wT_copied"], 1)
                nc.scalar.activation(wkT[:, :], s_ps[0][:, P:2 * P], ACT.Copy).then_inc(S["wT_copied"], 1)
                nc.scalar.activation(wvT[:, :], s_ps[0][:, 2 * P:3 * P], ACT.Copy).then_inc(S["wT_copied"], 1)
                act.wait_ge(S["gu_ready"], g + 1)
                for h in range(2):
                    last = nc.scalar.activation(gu_at(g, 0, h), gu_ps[h], ACT.Copy)
                last.then_inc(S["guhi_done"], 1)
            def hi_of_xn(m):
                for q in range(SPLIT):
                    b = m * SPLIT + q
                    seen(act, S["xn_done"], 4 * b + 4)
                    seen(act, S[f"xn_stored{q}"], 16 * m)
                    nc.scalar.activation(PT[:, 0, q * T:(q + 1) * T], xn_f32[:, q, :, :].rearrange("p t c -> p (t c)"),
                                         ACT.Copy).then_inc(S["xnhi_done"], 1)
                    act.wait_ge(S["xT_ready"], b + 1)
                    nc.scalar.activation(XT[:, 0, bass.ds(b * T, T)], pt_ps[:, q, :, :].rearrange("p t c -> p (t c)"),
                                         ACT.Copy).then_inc(S["xThi_done"], 1)

            hi_of_xn(0)
            with act.Fori(1, B // SPLIT) as m:
                hi_of_xn(m)

            def t_hi(n, h):
                seen(act, S["t_ready"], 2 * n + h + 1)
                seen(act, S["s_ready"], 8 * n)
                nc.scalar.activation(t_sb[:, 0, h, :], t_ps[:, :], ACT.Copy).then_inc(S["thi_done"], 1)

            def exps(n, i, h):
                seen(act, S["max_done"], 8 * n + 2 * i + h + 1)
                seen(act, S["inv_done"], NT * (n - 1) + i + 1)
                nc.scalar.activation(p_at(i, h), p_at(i, h), ACT.Exp, bias=neg_max[:, i, h:h + 1], scale=-1.0,
                                     accum_out=row_sum[:, i, h:h + 1]).then_inc(S["exp_done"], 1)

            def pt_hi(n, i):
                seen(act, S["pt_ready"], NT * n + i + 1)
                seen(act, S["y_ready"], 2 * (n - 1) + i // 2 + 1)
                o = pt_at(0, i // 2)
                nc.scalar.activation(o[:, 0:i + 1, :, i % 2, :].rearrange("p j h q -> p h j q"),
                                     pt_ps[:, :, 0:i + 1, :], ACT.Copy).then_inc(S["pthi_done"], 1)

            def y_hi(n, half):
                seen(act, S["y_ready"], 2 * n + half + 1)
                seen(act, S["out_ready"], 2 * n)
                nc.scalar.activation(y_sb[:, 0, :, half * 256:(half + 1) * 256], y_ps[:, :, :], ACT.Copy)\
                    .then_inc(S["yhi_done"], 1)

            def step(n, cur=True, prev=True, prev2=True, nxt=True):
                if prev:
                    pt_hi(n - 1, 0)
                if prev2:
                    y_hi(n - 2, 1)
                for i in range(2):
                    if prev:
                        pt_hi(n - 1, i + 1)
                    if cur:
                        exps(n, i, 0)
                        exps(n, i, 1)
                if prev:
                    pt_hi(n - 1, 3)
                if cur:
                    exps(n, 2, 0)
                    exps(n, 2, 1)
                if nxt:
                    t_hi(n + 1, 0)
                if prev:
                    y_hi(n - 1, 0)
                if cur:
                    exps(n, 3, 0)
                if nxt:
                    t_hi(n + 1, 1)
                if cur:
                    exps(n, 3, 1)

            def post_out(b):
                act.wait_ge(S["out_ready"], 16 * (b + 1))
                nc.scalar.activation(outT[:, :], out_ps[:, :], ACT.Copy).then_inc(S["outT_copied"], 1)

            t_hi(0, 0)
            t_hi(0, 1)
            step(0, prev=False, prev2=False)
            step(1, prev2=False)
            with act.Fori(2, 9) as n:
                step(n)
            def post_xn2T(b):
                seen(act, S["xn2T_ready"], b + 1)
                nc.scalar.activation(xn2T[:, :], post_ps[:, :], ACT.Copy).then_inc(S["xn2T_copied"], 1)
                seen(act, S["xn2_done"], 4 * b + 4)
                nc.scalar.activation(routed[:, 1, :, 0:C], routed[:, 0, :, 0:C], ACT.Copy).then_inc(S["rows_copied"], 1)

            def post_gap(b):
                seen(act, S["gap_done"], b + 1)
                nc.scalar.activation(gap_exp[:, :], gap[:, :], ACT.Exp).then_inc(S["gap_exp_done"], 1)

            with act.Fori(1, STEPS - 1 - NP) as v:
                step(v + NP)
                with act.If((v % NP) == 1):
                    post_out(v // NP)
                with act.If((v % NP) == 4):
                    post_xn2T(v // NP)
                with act.If((v % NP) == 5):
                    post_gap(v // NP)
            step(STEPS - 1, nxt=False)
            step(STEPS, cur=False, nxt=False)
            step(STEPS + 1, cur=False, prev=False, nxt=False)
            post_out(B - 1)
            post_xn2T(B - 1)
            post_gap(B - 1)

            act.wait_ge(S["ffn_up_in"], 32)
            act.wait_ge(S["g_loaded"], 16 * STEPS)
            act.wait_ge(S["u_loaded"], 16 * STEPS)
            for e in range(E):
                nc.scalar.activation(up_hi[:, e, :], W_ffn[:, e, :], ACT.Copy).then_inc(S["up_hi_done"], 1)

            def tile_xT(m, q):
                j = RING * m + q
                seen(act, S["x_tile_T"], j + 1)
                seen(act, S["u_ready"], j - 1)
                nc.scalar.activation(xT_tile[q % 2][:, 0, :], post_ps[:, 0:P], ACT.Copy).then_inc(S["x_hi"], 1)

            def tile_silu(m, q):
                j = RING * m + q
                seen(act, S["g_ready"], j + 1)
                seen(act, S["h_done"], j - 1)
                nc.scalar.activation(silu_sb[q % 2], g_ps[q % 2], ACT.Silu).then_inc(S["silu_done"], 1)

            def tile_hT(m, q):
                j = RING * m + q
                seen(act, S["hT_ready"], j + 1)
                seen(act, S["eo_ready"], j - 1)
                nc.scalar.activation(hT_sb[q % 2][:, :], out_ps[:, :], ACT.Copy).then_inc(S["hT_copied"], 1)

            def turn(m, q, first=False, last=False, drain=False):
                if not last and not drain:
                    tile_xT(*after(m, q))
                if not drain:
                    tile_silu(m, q)
                if not first:
                    tile_hT(*before(m, q))

            tile_xT(0, 0)
            for q in range(RING):
                turn(0, q, first=(q == 0))
            with act.Fori(1, TURNS) as m:
                for q in range(RING):
                    turn(m, q)
            for q in range(LEFT):
                turn(TURNS, q, last=(q == LEFT - 1))
            turn(TURNS, LEFT, drain=True)

        @block.vector
        def _(dve):
            dve.wait_ge(consts, 6)
            for t in range(TILES):
                if t % 8 == 0:
                    dve.wait_ge(x_in[t // 8], 16)
                nc.vector.bn_stats(stats[:, t, :], X[:, t, :]).then_inc(S["stats_done"], 1)
            for t in range(TILES):
                dve.wait_ge(S["stats_done"], t + 1)
                nc.vector.bn_aggr(mv[:, t, :], stats[:, t, :]).then_inc(S["aggr_done"], 1)
            for g in range(NP):
                dve.wait_ge(S["guhi_done"], g + 1)
                for h in range(2):
                    last = nc.vector.tensor_tensor(gu_at(g, 1, h), gu_ps[h], gu_at(g, 0, h).bitcast(F32), ALU.subtract)
                last.then_inc(S["gulo_done"], 1)
            dve.wait_ge(S["rstd_done"], 2)
            def normalise(m):
                for q in range(SPLIT):
                    b = m * SPLIT + q
                    seen(dve, S["xT_ready"], b - 1)
                    seen(dve, S["xnlo_done"], b - 1)
                    for t in range(NT):
                        nc.vector.tensor_scalar(xn_f32[:, q, t, :], X[:, bass.ds(4 * b + t, 1), :].rearrange("p a c -> p (a c)"),
                                                mv[:, bass.ds(4 * b + t, 1), 0], rstd[:, bass.ds(4 * b + t, 1)],
                                                ALU.subtract, ALU.mult).then_inc(S["xn_done"], 1)
                    dve.wait_ge(S["xnhi_done"], b + 1)
                    nc.vector.tensor_tensor(PT[:, 1, q * T:(q + 1) * T], xn_f32[:, q, :, :].rearrange("p t c -> p (t c)"),
                                            PT[:, 0, q * T:(q + 1) * T].bitcast(F32), ALU.subtract).then_inc(S["xnlo_done"], 1)
                    dve.wait_ge(S["xThi_done"], b + 1)
                    nc.vector.tensor_tensor(XT[:, 1, bass.ds(b * T, T)], pt_ps[:, q, :, :].rearrange("p t c -> p (t c)"),
                                            XT[:, 0, bass.ds(b * T, T)].bitcast(F32), ALU.subtract).then_inc(S["xTlo_done"], 1)

            normalise(0)
            with dve.Fori(1, B // SPLIT) as m:
                normalise(m)

            def t_lo(n, h):
                seen(dve, S["thi_done"], 2 * n + h + 1)
                nc.vector.tensor_tensor(t_sb[:, 1, h, :], t_ps[:, :], t_sb[:, 0, h, :].bitcast(F32), ALU.subtract)\
                    .then_inc(S["tlo_done"], 1)

            def maxes(n, i):
                seen(dve, S["s_ready"], 8 * n + 2 * i + 2)
                seen(dve, S["pt_ready"], NT * (n - 1) + i + 1)
                if i:
                    inv(n, i - 1)
                else:
                    inv(n - 1, NT - 1)
                w = P * (i + 1)
                for h in range(2):
                    nc.vector.tensor_tensor_reduce(out=p_at(i, h), in0=s_ps[h][:, 0:w], in1=mask[:, T - w:T],
                                                   scale=-SCALE, scalar=BIG, op0=ALU.add, op1=ALU.min,
                                                   accum_out=neg_max[:, i, h:h + 1]).then_inc(S["max_done"], 1)

            def inv(n, i):
                if isinstance(n, int) and n < 0:
                    return
                seen(dve, S["exp_done"], 8 * n + 2 * i + 2)
                if i < 2:
                    seen(dve, S["norm_dve"], 2 * (n - 1) + i + 1)
                else:
                    seen(dve, S["norm_pool"], 2 * (n - 1) + i - 2 + 1)
                nc.vector.reciprocal(row_inv[:, i, :], row_sum[:, i, :]).then_inc(S["inv_done"], 1)

            def norm(n, i):
                seen(dve, S["inv_done"], NT * n + i + 1)
                for h in range(2):
                    last = nc.vector.tensor_scalar(p_at(i, h), p_at(i, h), row_inv[:, i, h:h + 1], None, ALU.mult)
                last.then_inc(S["norm_dve"], 1)

            def pt_lo(n, i):
                seen(dve, S["pthi_done"], NT * n + i + 1)
                hi = pt_at(0, i // 2).bitcast(F32)[:, 0:i + 1, :, i % 2, :]
                lo = pt_at(1, i // 2)[:, 0:i + 1, :, i % 2, :]
                nc.vector.tensor_tensor(lo.rearrange("p j h q -> p h j q"), pt_ps[:, :, 0:i + 1, :],
                                        hi.rearrange("p j h q -> p h j q"), ALU.subtract).then_inc(S["ptlo_done"], 1)

            def y_lo(n, half):
                seen(dve, S["yhi_done"], 2 * n + half + 1)
                o = slice(half * 256, (half + 1) * 256)
                nc.vector.tensor_tensor(y_sb[:, 1, :, o], y_ps[:, :, :], y_sb[:, 0, :, o].bitcast(F32), ALU.subtract)\
                    .then_inc(S["ylo_done"], 1)

            def step(n, cur=True, prev=True, prev2=True, nxt=True):
                if prev:
                    pt_lo(n - 1, 0)
                if prev2:
                    y_lo(n - 2, 1)
                if cur:
                    maxes(n, 0)
                elif prev:
                    inv(n - 1, NT - 1)
                for i in range(1, 3):
                    if prev:
                        pt_lo(n - 1, i)
                    if cur:
                        maxes(n, i)
                if cur:
                    norm(n, 0)
                if prev:
                    pt_lo(n - 1, 3)
                if nxt:
                    t_lo(n + 1, 0)
                if cur:
                    maxes(n, 3)
                if prev:
                    y_lo(n - 1, 0)
                if nxt:
                    t_lo(n + 1, 1)
                if cur:
                    norm(n, 1)

            def post_x2(b):
                seen(dve, S["outT_ready"], b + 1)
                xs = X[:, bass.ds(4 * b, 4), :].rearrange("p a c -> p (a c)")
                nc.vector.tensor_tensor(xs, post_ps[:, :], xs, ALU.add).then_inc(S["x2_done"], 1)
                seen(dve, S["x2_done"], b + 1)
                nc.vector.tensor_scalar(dest[:, :, :], dest[:, :, :], float(T), None, ALU.add).then_inc(S["dest_done"], 1)
                for t in range(NT):
                    nc.vector.bn_stats(stats[:, t, :], X[:, bass.ds(4 * b + t, 1), :].rearrange("p a c -> p (a c)"))\
                        .then_inc(S["stats2"], 1)
                seen(dve, S["stats2"], 8 * b + 4)
                nc.vector.memset(gate_v[:, :], 0)
                for t in range(NT):
                    nc.vector.bn_aggr(mv[:, t, :], stats[:, t, :]).then_inc(S["stats2"], 1)

            def post_xn2(b):
                seen(dve, S["rstd2"], 2 * b + 2)
                seen(dve, S["rows_written"], 16 * (K * NT * b + 1))
                for t in range(NT):
                    nc.vector.tensor_scalar(routed[:, 0, t, 0:C], X[:, bass.ds(4 * b + t, 1), :].rearrange("p a c -> p (a c)"),
                                            mv[:, t, 0:1], rstd[:, t:t + 1], ALU.subtract, ALU.mult).then_inc(S["xn2_done"], 1)

            ROUTING = 21

            def post_choose(b):
                def made(k):
                    seen(dve, S["routing"], ROUTING * b + k)

                def sig(ins):
                    ins.then_inc(S["routing"], 1)

                seen(dve, S["logits_ready"], b + 1)
                sig(nc.vector.tensor_copy(logit[:, :, :].rearrange("p t e -> p (t e)"), post_ps[:, 0:NT * E]))
                for t in range(NT):
                    sig(nc.vector.max(top[:, t, :], post_ps[:, t * E:(t + 1) * E]))
                made(5)
                nc.vector.tensor_tensor(gap[:, :], top[:, :, 1], top[:, :, 0], ALU.subtract).then_inc(S["gap_done"], 1)
                for t in range(NT):
                    sig(nc.vector.max_index(top_i[:, t, :], top[:, t, :], logit[:, t, :]))
                made(9)
                sig(nc.vector.tensor_copy(top_f[:, :, :], top_i[:, :, 0:K]))
                made(10)
                for k in range(K):
                    sig(nc.vector.tensor_tensor(chosen[:, k, :, :], expert_id[:, :, :],
                                                top_f[:, :, k].unsqueeze(2).to_broadcast([P, NT, E]), ALU.is_equal))
                made(12)
                nc.vector.tensor_tensor(chosen_bf[:, :, :], chosen[:, 0, :, :], chosen[:, 1, :, :], ALU.add)\
                    .then_inc(S["chosen_done"], 1)

            def post_rows(b):
                def made(k):
                    seen(dve, S["routing"], ROUTING * b + k)

                def sig(ins):
                    ins.then_inc(S["routing"], 1)

                seen(dve, S["ranks_ready"], b + 1)
                sig(nc.vector.tensor_tensor(pos[:, :, :], post_ps[:, RANK_COL:RANK_COL + NT * E].rearrange("p (t e) -> p t e", e=E),
                                            base[:, :].unsqueeze(1).to_broadcast([P, NT, E]), ALU.add))
                made(13)
                sig(nc.vector.tensor_tensor(base[:, :], post_ps[:, TOTAL_COL:TOTAL_COL + E], base[:, :], ALU.add))
                for k in range(K):
                    sig(nc.vector.tensor_tensor(picked[:, k, :, :], chosen[:, k, :, :], pos[:, :, :], ALU.mult))
                made(16)
                sig(nc.vector.tensor_reduce(row_f[:, :, :], picked[:, :, :, :], AX.X, ALU.add))
                seen(dve, S["gap_exp_done"], b + 1)
                sig(nc.vector.tensor_scalar(weight[:, 1, :], gap_exp[:, :], 1.0, None, ALU.add))
                made(18)
                sig(nc.vector.reciprocal(weight[:, 0, :], weight[:, 1, :]))
                sig(nc.vector.tensor_copy(row_i[:, :, :], row_f[:, :, :]))
                made(19)
                sig(nc.vector.tensor_tensor(weight[:, 1, :], gap_exp[:, :], weight[:, 0, :], ALU.mult))
                made(21)
                nc.vector.tensor_scalar(routed[:, :, :, C], weight[:, :, :], DEPTH_SCALE, None, ALU.mult)
                seen(dve, S["rows_copied"], b + 1)
                seen(dve, S["dest_done"], b + 1)
                nc.vector.tensor_copy(routed[:, :, :, C + 1], dest[:, :, :]).then_inc(S["rows_done"], 1)

            nc.vector.tensor_scalar(base[:, :], expert_id[:, 0, :], float(REGION), None, ALU.mult).then_inc(S["base_set"], 1)
            dve.wait_ge(S["base_set"], 1)
            t_lo(0, 0)
            t_lo(0, 1)
            step(0, prev=False, prev2=False)
            step(1, prev2=False)
            with dve.Fori(2, 9) as n:
                step(n)
            with dve.Fori(1, STEPS - 1 - NP) as v:
                step(v + NP)
                with dve.If((v % NP) == 2):
                    post_x2(v // NP)
                with dve.If((v % NP) == 3):
                    post_xn2(v // NP)
                with dve.If((v % NP) == 5):
                    post_choose(v // NP)
                with dve.If((v % NP) == 6):
                    post_rows(v // NP)
            step(STEPS - 1, nxt=False)
            step(STEPS, cur=False, nxt=False)
            step(STEPS + 1, cur=False, prev=False, nxt=False)
            post_x2(B - 1)
            post_xn2(B - 1)
            post_choose(B - 1)
            post_rows(B - 1)

            tabled = [0]

            def tab(ins):
                tabled[0] += 1
                ins.then_inc(S["tabling"], 1)
                dve.wait_ge(S["tabling"], tabled[0])

            tab(nc.vector.scalar_tensor_tensor(count[:, :], expert_id[0:1, 0, :], float(-REGION), base[0:1, :], ALU.mult, ALU.add))
            tab(nc.vector.tensor_scalar(count_i[:, :], count[:, :], float(P - 1), None, ALU.add))
            tab(nc.vector.tensor_single_scalar(count_i[:, :], count_i[:, :], 7, op=ALU.arith_shift_right))
            tab(nc.vector.tensor_copy(tiles_of[:, :], count_i[:, :]))
            tab(nc.vector.tensor_copy(ends[:, :], tiles_of[:, :]))
            for e in range(1, E):
                tab(nc.vector.tensor_tensor(ends[:, e:e + 1], ends[:, e - 1:e], ends[:, e:e + 1], ALU.add))
            tab(nc.vector.tensor_scalar(jump[:, :], tiles_of[:, :], float(-P), float(REGION), ALU.mult, ALU.add))
            shape = [1, SLOTS, E - 1]
            tab(nc.vector.tensor_tensor(past[:, :, :], slot_id[0:1, :].unsqueeze(2).to_broadcast(shape),
                                        ends[:, 0:E - 1].unsqueeze(1).to_broadcast(shape), ALU.is_ge))
            tab(nc.vector.tensor_tensor(jumps[:, :, :], past[:, :, :], jump[:, 0:E - 1].unsqueeze(1).to_broadcast(shape), ALU.mult))
            tab(nc.vector.tensor_reduce(table_f[:, 0, :], past[:, :, :], AX.X, ALU.add))
            tab(nc.vector.tensor_reduce(table_f[:, 1, :], jumps[:, :, :], AX.X, ALU.add))
            tab(nc.vector.scalar_tensor_tensor(table_f[:, 1, :], slot_id[0:1, :], float(P), table_f[:, 1, :], ALU.mult, ALU.add))
            tab(nc.vector.tensor_scalar(table_f[:, 1, :], table_f[:, 1, :], float(E * REGION - P), None, ALU.min))
            nc.vector.tensor_copy(table[:, :, :], table_f[:, :, :]).then_inc(S["table_done"], 1)

            dve.wait_ge(S["s_ready"], 8 * STEPS)
            for e in range(E):
                dve.wait_ge(S["up_hi_done"], e + 1)
                nc.vector.tensor_tensor(up_lo[:, e, :], W_ffn[:, e, :], up_hi[:, e, :].bitcast(F32), ALU.subtract)\
                    .then_inc(S["up_lo_done"], 1)

            def tile_xT(m, q):
                j = RING * m + q
                seen(dve, S["x_hi"], j + 1)
                nc.vector.tensor_tensor(xT_tile[q % 2][:, 1, :], post_ps[:, 0:P], xT_tile[q % 2][:, 0, :].bitcast(F32), ALU.subtract)\
                    .then_inc(S["x_lo"], 1)

            def tile_meta(m, q):
                j = RING * m + q
                seen(dve, S[f"x_tile_in{q}"], 16 * (m + 1))
                seen(dve, S["gated"], j - RING + 1)
                seen(dve, S[f"eo_out{q}"], 16 * m)
                nc.vector.tensor_copy(meta_w[:, q:q + 1], x_in_tile[q][:, C:C + 1]).then_inc(S["meta_done"], 1)
                nc.vector.tensor_scalar(meta_row[:, q:q + 1], x_in_tile[q][:, C + 1:C + 2], -1.0, None, ALU.add)\
                    .then_inc(S["meta_done"], 1)

            def tile_h(m, q):
                j = RING * m + q
                seen(dve, S["silu_done"], j + 1)
                seen(dve, S["u_ready"], j + 1)
                seen(dve, S["hT_ready"], j - 1)
                nc.vector.tensor_tensor(h_sb[q % 2], u_ps[q % 2], silu_sb[q % 2], ALU.mult).then_inc(S["h_done"], 1)

            def tile_eo(m, q):
                j = RING * m + q
                seen(dve, S["eo_ready"], j + 1)
                seen(dve, S["meta_done"], 2 * (j + 1))
                seen(dve, S[f"eo_out{(q - 2) % RING}"], 16 * (m + 1) if q >= 2 else 16 * m)
                nc.vector.tensor_scalar(eo_sb[q % 2], eo_ps[q % 2], meta_w[:, q:q + 1], None, ALU.mult).then_inc(S["eo_done"], 1)

            def turn(m, q, first=False, last=False, drain=False):
                if not last and not drain:
                    tile_xT(*after(m, q))
                    tile_meta(*after(m, q))
                if not drain:
                    tile_h(m, q)
                if not first:
                    tile_eo(*before(m, q))

            tile_xT(0, 0)
            tile_meta(0, 0)
            for q in range(RING):
                turn(0, q, first=(q == 0))
            with dve.Fori(1, TURNS) as m:
                for q in range(RING):
                    turn(m, q)
            for q in range(LEFT):
                turn(TURNS, q, last=(q == LEFT - 1))
            turn(TURNS, LEFT, drain=True)

            n = TILES // 4
            for k in range(4):
                xs = X[:, k * n:(k + 1) * n, :]
                dve.wait_ge(back_in[k], 32)
                nc.vector.tensor_tensor(xs, back[:, 0, k * n:(k + 1) * n, :], xs, ALU.add).then_inc(S["added"], 1)
                dve.wait_ge(S["added"], 2 * k + 1)
                nc.vector.tensor_tensor(xs, back[:, 1, k * n:(k + 1) * n, :], xs, ALU.add).then_inc(S["added"], 1)

        @block.tensor
        def _(pe):
            pe.wait_ge(consts, 6)
            pe.wait_ge(w_in, 64)
            nc.tensor.transpose(post_ps[:, 0:P], w_down_sb, ident[:, :]).then_inc(S["wdT_ready"], 1)
            pe.wait_ge(S["wdT_copied"], 1)
            for g in range(NP):
                d = slice(g * P, (g + 1) * P)
                if g:
                    pe.wait_ge(S["wT_copied"], 3 * g)
                nc.tensor.transpose(s_ps[0][:, 0:P], w_q_sb[:, d], ident[:, :])
                nc.tensor.matmul(s_ps[0][:, P:2 * P], w_up_sb[:, g * P:(g + 1) * P], wdT[:, :], start=True, stop=True)
                nc.tensor.matmul(s_ps[0][:, 2 * P:3 * P], w_up_sb[:, NH * HD + g * P:NH * HD + (g + 1) * P], wdT[:, :],
                                 start=True, stop=True).then_inc(S["wqT_ready"], 1)
                pe.wait_ge(S["wT_copied"], 3 * g + 3)
                if g:
                    pe.wait_ge(S["gulo_done"], g)
                for h in range(2):
                    k = slice(h * HD, (h + 1) * HD)
                    nc.tensor.matmul(gu_ps[h][:, 0, :], wqT[k, :], wkT[k, :], start=True, stop=True)
                    last = nc.tensor.matmul(gu_ps[h][:, 1, :], wvT[k, :], w_out_sb[k, g, :], start=True, stop=True)
                last.then_inc(S["gu_ready"], 1)
            def transpose_xn(m):
                for q in range(SPLIT):
                    b = m * SPLIT + q
                    pe.wait_ge(S["xn_done"], 4 * b + 4)
                    seen(pe, S["xTlo_done"], b - 1)
                    for t in range(NT):
                        last = nc.tensor.transpose(pt_ps[:, q, t, :], xn_f32[:, q, t, :], ident[:, :])
                    last.then_inc(S["xT_ready"], 1)

            transpose_xn(0)
            with pe.Fori(1, B // SPLIT) as m:
                transpose_xn(m)

            def passes(dst, ws, vs, start, stop, **kw):
                nc.tensor.matmul(dst, ws[0], vs[0], start=start, stop=False, **kw)
                nc.tensor.matmul(dst, ws[1], vs[0], start=False, stop=False, **kw)
                return nc.tensor.matmul(dst, ws[0], vs[1], start=False, stop=stop, **kw)

            def xT_at(part, b, w):
                return XT[:, part, bass.ds(b * T, w)]

            def project(n, h):
                seen(pe, S["g_loaded"], 16 * (n + 1))
                seen(pe, S["tlo_done"], 2 * n + h)
                b = n // NP
                passes(t_ps[:, :], [G_cur[:, a, h, :] for a in range(2)], [xT_at(a, b, T) for a in range(2)],
                       True, True).then_inc(S["t_ready"], 1)

            def scores(n, i):
                w = max(256, P * (i + 1))
                b = n // NP
                for h in range(2):
                    if i == 0:
                        seen(pe, S["tlo_done"], 2 * n + h + 1)
                    seen(pe, S["max_done"], 8 * n + 2 * i + h - 1)
                    passes(s_ps[h][:, 0:w], [t_sb[:, a, h, i * P:(i + 1) * P] for a in range(2)],
                           [xT_at(a, b, w) for a in range(2)], True, True).then_inc(S["s_ready"], 1)

            def transposes(n, i):
                if i < 2:
                    seen(pe, S["norm_dve"], 2 * n + i + 1)
                else:
                    seen(pe, S["norm_pool"], 2 * n + i - 2 + 1)
                seen(pe, S["ptlo_done"], NT * n + i)
                for h in range(2):
                    for j in range(i + 1):
                        last = nc.tensor.transpose(pt_ps[:, h, j, :], p_at(i, h)[:, j * P:(j + 1) * P], ident[:, :])
                last.then_inc(S["pt_ready"], 1)

            def values(n, half):
                seen(pe, S["ptlo_done"], NT * n + 2 * half + 2)
                seen(pe, S["ylo_done"], 2 * n + half)
                seen(pe, S["xn_loaded"], 16 * (n // NP + 1))
                keys = 2 * half + 2
                for j in range(keys):
                    if j < keys - 1:
                        dst = y_ps[:, :, :].rearrange("p h q -> p (h q)")
                        src = [pt_at(a, half)[:, j, :, :, :].rearrange("p h i q -> p (h i q)") for a in range(2)]
                    else:
                        dst = y_ps[:, :, P:256]
                        src = [pt_at(a, half)[:, j, :, 1, :] for a in range(2)]
                    last = passes(dst, [xn_cur[:, a, j, :] for a in range(2)], src, j == 0, j == keys - 1)
                last.then_inc(S["y_ready"], 1)

            def project_out(n, h):
                if h == 0:
                    seen(pe, S["u_loaded"], 16 * (n + 1))
                    seen(pe, S["ylo_done"], 2 * n + 2)
                passes(out_ps[:, :], [U_cur[:, a, h, :] for a in range(2)], [y_sb[:, a, h, :] for a in range(2)],
                       False, True, skip_group_check=True).then_inc(S["out_ready"], 1)

            def clear_out():
                nc.tensor.matmul(out_ps[:, :], zero_bf[:, 0:P], zero_bf[:, :], start=True, stop=True)

            def step(n, cur=True, prev=True, prev2=True, nxt=True):
                if prev:
                    transposes(n - 1, 0)
                if prev2:
                    values(n - 2, 1)
                if cur:
                    scores(n, 0)
                if prev:
                    transposes(n - 1, 1)
                if cur:
                    scores(n, 1)
                if prev2:
                    project_out(n - 2, 0)
                if prev:
                    transposes(n - 1, 2)
                if cur:
                    scores(n, 2)
                if prev2:
                    project_out(n - 2, 1)
                if prev:
                    transposes(n - 1, 3)
                if cur:
                    scores(n, 3)
                if nxt:
                    project(n + 1, 0)
                if prev:
                    values(n - 1, 0)
                if nxt:
                    project(n + 1, 1)

            def post_out(b):
                pe.wait_ge(S["outT_copied"], b + 1)
                clear_out()
                for t in range(NT):
                    last = nc.tensor.transpose(post_ps[:, t * P:(t + 1) * P], outT[:, t * P:(t + 1) * P], ident[:, :])
                last.then_inc(S["outT_ready"], 1)

            def post_xn2T(b):
                seen(pe, S["xn2_done"], 4 * b + 4)
                seen(pe, S["x2_done"], b + 1)
                for t in range(NT):
                    last = nc.tensor.transpose(post_ps[:, t * P:(t + 1) * P], routed[:, 0, t, 0:C], ident[:, :])
                last.then_inc(S["xn2T_ready"], 1)

            def post_logits(b):
                pe.wait_ge(S["wr_in"], 16)
                seen(pe, S["xn2T_copied"], b + 1)
                for t in range(NT):
                    last = nc.tensor.matmul(post_ps[:, t * E:(t + 1) * E], xn2T[:, t * P:(t + 1) * P], Wr_sb[:, :],
                                            start=True, stop=True)
                last.then_inc(S["logits_ready"], 1)

            def post_ranks(b):
                seen(pe, S["chosen_done"], b + 1)
                ranks = post_ps[:, RANK_COL:RANK_COL + NT * E].rearrange("p (t e) -> p t e", e=E)
                total = post_ps[:, TOTAL_COL:TOTAL_COL + E]
                kw = dict(skip_group_check=True)
                nc.tensor.matmul(ranks, before_bf[:, :], chosen_bf[:, :, :], start=True, stop=True, **kw)
                for t in range(NT - 1):
                    nc.tensor.matmul(ranks[:, t + 1:NT, :], ones_bf[:, :],
                                     chosen_bf[:, t:t + 1, :].to_broadcast([P, NT - 1 - t, E]), start=False, stop=True, **kw)
                for t in range(NT):
                    last = nc.tensor.matmul(total, ones_bf[:, :], chosen_bf[:, t, :], start=False, stop=True, **kw)
                last.then_inc(S["ranks_ready"], 1)

            pe.wait_ge(S["xTlo_done"], B)
            clear_out()
            project(0, 0)
            project(0, 1)
            step(0, prev=False, prev2=False)
            step(1, prev2=False)
            with pe.Fori(2, 9) as n:
                step(n)
            with pe.Fori(1, STEPS - 1 - NP) as v:
                step(v + NP)
                with pe.If((v % NP) == 1):
                    post_out(v // NP)
                with pe.If((v % NP) == 3):
                    post_xn2T(v // NP)
                with pe.If((v % NP) == 4):
                    post_logits(v // NP)
                with pe.If((v % NP) == 5):
                    post_ranks(v // NP)
            step(STEPS - 1, nxt=False)
            step(STEPS, cur=False, nxt=False)
            step(STEPS + 1, cur=False, prev=False, nxt=False)
            post_out(B - 1)
            post_xn2T(B - 1)
            post_logits(B - 1)
            post_ranks(B - 1)

            def tile_xT(m, q):
                j = RING * m + q
                seen(pe, S[f"x_tile_in{q}"], 16 * (m + 1))
                seen(pe, S["x_lo"], j)
                nc.tensor.transpose(post_ps[:, 0:P], x_in_tile[q][:, 0:C], ident[:, :]).then_inc(S["x_tile_T"], 1)

            def tile_up(j, q, e, half):
                dst, o = (g_ps[q % 2], 0) if half == 0 else (u_ps[q % 2], HID)
                return passes(dst, [xT_tile[q % 2][:, a, :] for a in range(2)],
                              [w[:, bass.ds(e, 1), o:o + HID].rearrange("p a n -> p (a n)") for w in (up_hi, up_lo)], True, True)

            def tile_g(m, q, e):
                j = RING * m + q
                seen(pe, S["x_lo"], j + 1)
                seen(pe, S["h_done"], j - 1)
                tile_up(j, q, e, 0).then_inc(S["g_ready"], 1)

            def tile_u(m, q, e):
                tile_up(2 * m + q, q, e, 1).then_inc(S["u_ready"], 1)

            def tile_hT(m, q):
                j = RING * m + q
                seen(pe, S["h_done"], j + 1)
                seen(pe, S["hT_copied"], j)
                for k in range(HC):
                    last = nc.tensor.transpose(out_ps[:, k * P:(k + 1) * P], h_sb[q % 2][:, k * P:(k + 1) * P], ident[:, :])
                last.then_inc(S["hT_ready"], 1)

            def tile_down(m, q, e):
                j = RING * m + q
                seen(pe, S["hT_copied"], j + 1)
                seen(pe, S["eo_done"], j - 1)
                for k in range(HC):
                    last = nc.tensor.matmul(eo_ps[q % 2], hT_sb[q % 2][:, k * P:(k + 1) * P],
                                            W_dn[:, bass.ds(e, 1), k, :].rearrange("p a c -> p (a c)"),
                                            start=(k == 0), stop=(k == HC - 1))
                last.then_inc(S["eo_ready"], 1)

            expert_reg = [nc.tensor.alloc_register(f"expert{q}") for q in range(RING)]

            def load_expert(m, q):
                nc.tensor.reg_load(expert_reg[q], table[0:1, 0, bass.ds(RING * m + q, 1)])

            def expert(q):
                return nc.tensor.snap(expert_reg[q], min_val=0, max_val=E - 1)

            def turn(m, q, first=False, last=False, drain=False):
                if not last and not drain:
                    tile_xT(*after(m, q))
                if not drain:
                    e = expert(q)
                    tile_g(m, q, e)
                if not first:
                    tile_hT(*before(m, q))
                if not drain:
                    tile_u(m, q, e)
                if not last and not drain:
                    load_expert(*after(m, q))
                if not first:
                    tile_down(*before(m, q), expert((q - 1) % RING))

            pe.wait_ge(S["table_done"], 1)
            pe.wait_ge(S["up_lo_done"], E)
            pe.wait_ge(S["ffn_down_in"], 16)
            load_expert(0, 0)
            tile_xT(0, 0)
            for q in range(RING):
                turn(0, q, first=(q == 0))
            with pe.Fori(1, TURNS) as m:
                for q in range(RING):
                    turn(m, q)
            for q in range(LEFT):
                turn(TURNS, q, last=(q == LEFT - 1))
            turn(TURNS, LEFT, drain=True)


_INS = {"L0_attn_x": (NTOK, C), "L0_attn_w_kv_down": None, "L0_attn_w_kv_up": None, "L0_attn_w_q": None,
        "L0_attn_w_out": None, "L0_ffn_Wr": None, "L0_ffn_Wg": None, "L0_ffn_Wu": None, "L0_ffn_Wd": None}


def kernel(**inputs):
    import concourse.bacc as bacc
    from concourse.bass_utils import run_bass_kernel_spmd

    nc = bacc.Bacc("TRN2", target_bir_lowering=False, num_devices=1)
    arrays, args = {}, []
    for name, shape in _INS.items():
        a = np.ascontiguousarray(inputs[name])
        a = a.reshape(shape) if shape else a
        arrays[f"in_{name}"] = a
        args.append(nc.dram_tensor(f"in_{name}", a.shape, mybir.dt.from_np(a.dtype), kind="ExternalInput").ap())
    args.append(nc.dram_tensor("out_0", (NTOK, C), F32, kind="ExternalOutput").ap())
    layer(nc, *args)
    r = run_bass_kernel_spmd(nc, [arrays], core_ids=[0])
    return r.results[0]["out_0"].reshape(B, T, C)
```

```python
from contextlib import ExitStack

import numpy as np
import concourse.bass as bass
from concourse import mybir

F32 = mybir.dt.float32
F32R = mybir.dt.float32r
BF16 = mybir.dt.bfloat16
I32 = mybir.dt.int32
U32 = mybir.dt.uint32
ALU = mybir.AluOpType
ACT = mybir.ActivationFunctionType
AX = mybir.AxisListType

P = 128
B, T, C = 8, 512, 128
NT = T // P
NH, HD = 16, 64
NP = NH // 2
R = 128
NTOK = B * T
TILES = NTOK // P
RING = 4
E, HID, K = 8, 512, 2
HC = HID // P
STEPS = B * NP
REGION = NTOK
ROW = C + 2
SLOTS = (NTOK * K + E * (P - 1)) // P
TURNS, LEFT = divmod(SLOTS, RING)
SCALE = HD ** -0.5
DEPTH_SCALE = 12 ** -0.5
EPS = 1e-5
MASKED = -1e30
BIG = 3e38
RANK_COL, TOTAL_COL = 64, 128


def seen(eng, sem, count):
    if not isinstance(count, int) or count > 0:
        eng.wait_ge(sem, count)


def before(m, q):
    return (m, q - 1) if q else (m - 1, RING - 1)


def after(m, q):
    return (m, q + 1) if q < RING - 1 else (m + 1, 0)


def layer(nc, x, w_down, w_up, w_q, w_out, Wr, Wg, Wu, Wd, out):
    ctx = ExitStack()
    with ctx:
        def sb(name, shape, dt=F32):
            return ctx.enter_context(nc.sbuf_tensor(name, shape, dt))

        def sem(name):
            return ctx.enter_context(nc.semaphore(name))

        xn_dram = nc.dram_tensor("xn_scratch", [B, P, 2 * T], F32).ap()
        rows_dram = nc.dram_tensor("routed_rows", [E * REGION, ROW], F32).ap()
        expert_dram = nc.dram_tensor("expert_out", [K * NTOK, C], F32).ap()

        X = sb("X", [P, TILES, C])
        XT = sb("XT", [P, 2, NTOK], F32R)
        GU = sb("GU", [P, NP, 1024], F32R)
        W_ffn = sb("W_ffn", [P, E, 2 * HID])
        W_dn = sb("W_dn", [P, E, HC, C])
        prob = sb("prob", [P, 2 * 1280])
        PT = sb("PT", [P, 2, 3072], F32R)
        t_sb = sb("t_sb", [P, 2, 2, T], F32R)
        y_sb = sb("y_sb", [P, 2, 2, T], F32R)
        G_cur = sb("G_cur", [P, 2, 2, P], F32R)
        U_cur = sb("U_cur", [P, 2, 2, P], F32R)
        xn_cur = sb("xn_cur", [P, 2, NT, C], F32R)
        mask = sb("mask", [P, T])
        ident = sb("ident", [P, P])
        zero_bf = sb("zero_bf", [P, T], BF16)
        wdT = sb("wdT", [P, P])
        wqT = sb("wqT", [P, P])
        wkT = sb("wkT", [P, P])
        wvT = sb("wvT", [P, P])
        row_sum = sb("row_sum", [P, NT, 2])
        row_inv = sb("row_inv", [P, NT, 2])
        neg_max = sb("neg_max", [P, NT, 2])
        stats = sb("stats", [P, TILES, 6])
        mv = sb("mv", [P, TILES, 2])
        rstd = sb("rstd", [P, TILES])
        power = sb("power", [P, TILES])
        eps = sb("eps", [P, NT])
        outT = sb("outT", [P, T])
        Wr_sb = sb("Wr_sb", [P, E])
        routed = sb("routed", [P, K, NT, ROW])
        xn2T = sb("xn2T", [P, T])
        before_bf = sb("before_bf", [P, P], BF16)
        ones_bf = sb("ones_bf", [P, P], BF16)
        const_i = sb("const_i", [P, P], I32)
        expert_id = sb("expert_id", [P, NT, E])
        slot_id = sb("slot_id", [P, SLOTS])
        dest = sb("dest", [P, K, NT])
        logit = sb("logit", [P, NT, E])
        top = sb("top", [P, NT, 8])
        top_i = sb("top_i", [P, NT, 8], U32)
        top_f = sb("top_f", [P, NT, K])
        chosen = sb("chosen", [P, K, NT, E])
        chosen_bf = sb("chosen_bf", [P, NT, E], BF16)
        gap = sb("gap", [P, NT])
        gap_exp = sb("gap_exp", [P, NT])
        weight = sb("weight", [P, K, NT])
        base = sb("base", [P, E])
        pos = sb("pos", [P, NT, E])
        picked = sb("picked", [P, K, NT, E])
        row_f = sb("row_f", [P, K, NT])
        row_i = sb("row_i", [P, K, NT], I32)
        count = sb("count", [1, E])
        count_i = sb("count_i", [1, E], I32)
        tiles_of = sb("tiles_of", [1, E])
        ends = sb("ends", [1, E])
        jump = sb("jump", [1, E])
        past, jumps = (prob[0:1, o:o + SLOTS * (E - 1)].rearrange("p (j e) -> p j e", e=E - 1) for o in (0, T))
        table_f = sb("table_f", [1, 2, SLOTS])
        table = sb("table", [1, 2, SLOTS], I32)
        gate_v = sb("gate_v", [P, 1], I32)
        gate_p = sb("gate_p", [P, RING + 1])
        meta_w = sb("meta_w", [P, RING])
        meta_row = sb("meta_row", [P, RING], I32)
        up_hi = GU[:, :, :]
        up_lo = XT[:, :, :].rearrange("p a n -> p (a n)").rearrange("p (e n) -> p e n", e=E)
        x_in_tile = [routed[:, 0, q, :] for q in range(RING)]
        xT_tile = [t_sb[:, q, :, 0:P] for q in range(2)]
        silu_sb = [prob[:, q * T:(q + 1) * T] for q in range(2)]
        h_sb = [prob[:, (2 + q) * T:(3 + q) * T] for q in range(2)]
        hT_sb = [outT, xn2T]
        eo_sb = [prob[:, 4 * T + q * C:4 * T + (q + 1) * C] for q in range(2)]
        back = W_ffn[:, :, :].rearrange("p e n -> p (e n)").rearrange("p (k t c) -> p k t c", k=K, c=C)

        w_up_sb = W_ffn[:, 0:2, :].rearrange("p a n -> p (a n)")
        w_q_sb = W_ffn[:, 2, :]
        w_out_sb = W_ffn[:, 3, :].rearrange("p (g c) -> p g c", g=NP)
        w_down_sb = W_ffn[:, 4, 0:R]
        xn_f32 = prob[:, 0:2 * T].rearrange("p (q t c) -> p q t c", q=2, c=C)

        s_ps = [ctx.enter_context(nc.psum_tensor(f"s_ps{h}", [P, T], F32)) for h in range(2)]
        bank_a, bank_b, bank_c, bank_d = (ctx.enter_context(nc.psum_tensor(f"bank_{k}", [P, T], F32)) for k in "abcd")
        pt_ps = [bank_a, bank_c, bank_a, bank_b, bank_d, bank_c]
        t_ps = [bank_a, bank_d]
        y_ps = bank_b
        out_ps = ctx.enter_context(nc.psum_tensor("out_ps", [P, T], F32))
        post_ps = ctx.enter_context(nc.psum_tensor("post_ps", [P, T], F32))

        gu_ps = [ps[:, 0:256].rearrange("p (k c) -> p k c", k=2) for ps in (s_ps[1], bank_d)]

        g_ps = [s_ps[0][:, :], bank_d[:, :]]
        u_ps = [s_ps[1][:, :], bank_c[:, :]]
        eo_ps = [bank_a[:, 0:P], bank_b[:, 0:P]]

        xT_ps = [bank_a[:, :], bank_b[:, :]]

        PARTS = [(0, None), (1, None), (2, 0), (2, 1), (3, 0), (3, 1)]
        NPT = len(PARTS)
        parts_to = [1, 2, 4, 6]

        def gu_at(g, part, h):
            return GU[:, g, :].rearrange("p (k a h c) -> p k a h c", k=2, a=2, h=2)[:, :, part, h, :]

        def p_pair(i):
            o = P * i * (i + 1)
            return prob[:, o:o + 2 * P * (i + 1)].rearrange("p (h k) -> p h k", h=2)

        def p_at(i, h):
            o = 128 * i * (i + 1) + h * 128 * (i + 1)
            return prob[:, o:o + 128 * (i + 1)]

        def pt_at(part, half):
            v = PT[:, part, 0:1024] if half == 0 else PT[:, part, 1024:3072]
            return v.rearrange("p (j h i q) -> p j h i q", h=2, i=2, q=P)

        def pt_part(u, part=None):
            i, h = PARTS[u]
            if part is None:
                v = pt_ps[u][:, 0:(i + 1) * P * (2 if h is None else 1)]
                return v.rearrange("p (h j q) -> p h j q", h=2, q=P) if h is None else v.rearrange("p (j q) -> p j q", q=P)
            v = pt_at(part, i // 2)[:, 0:i + 1, :, i % 2, :]
            return v.rearrange("p j h q -> p h j q") if h is None else v[:, :, h, :]

        x_in = [sem(f"x_in{k}") for k in range(4)]
        w_in = sem("w_in")
        consts = sem("consts")
        S = {n: sem(n) for n in (
            "stats_done", "aggr_done", "rstd_done", "xn_done", "xnhi_done", "xnlo_done", "xn_stored0", "xn_stored1", "xT_ready", "xThi_done", "xTlo_done",
            "wdT_ready", "wdT_copied", "wqT_ready", "wkT_ready", "wvT_ready", "wT_copied", "gu_ready", "guhi_done", "gulo_done",
            "g_loaded", "u_loaded", "xn_loaded",
            "t_ready", "thi_done", "tlo_done", "s_ready", "max_done", "exp_done", "inv_done", "norm_dve", "norm_pool",
            "pt_ready", "pthi_done", "ptlo_done", "y_ready", "yhi_done", "ylo_done", "out_ready",
            "outT_copied", "outT_ready", "x2_done", "stats2", "rstd2", "xn2_done", "xn2T_ready", "xn2T_copied", "rows_copied",
            "logits_ready", "routing", "chosen_done", "gap_done", "gap_exp_done", "ranks_ready", "rows_done", "rows_written", "dest_done", "base_set", "gated",
            "wr_in", "zero_tile", "ffn_up_in", "ffn_down_in", "table_done", "tabling", "up_hi_done", "up_lo_done",
            "x_tile_in0", "x_tile_in1", "x_tile_in2", "x_tile_in3", "x_tile_T", "x_hi", "x_lo", "meta_done", "g_ready", "u_ready", "silu_done", "h_done",
            "hT_ready", "hT_copied", "eo_ready", "eo_done", "eo_out0", "eo_out1", "eo_out2", "eo_out3", "added", "stored")}
        back_in = [sem(f"back_in{k}") for k in range(4)]

        block = ctx.enter_context(nc.Block())
        SPLIT = 2

        @block.sync
        def _(sp):
            sp.dma_start(w_down_sb, w_down).then_inc(w_in, 16)
            sp.dma_start(w_up_sb, w_up).then_inc(w_in, 16)
            sp.dma_start(w_q_sb, w_q).then_inc(w_in, 16)
            sp.dma_start(w_out_sb, w_out.rearrange("(g d) c -> d g c", d=P)).then_inc(w_in, 16)
            for k in range(4):
                n = TILES // 4
                sp.dma_start(X[:, k * n:(k + 1) * n, :],
                             x[k * n * P:(k + 1) * n * P, :].rearrange("(t p) c -> p t c", p=P)).then_inc(x_in[k], 16)
            sp.dma_start(Wr_sb[:, :], Wr).then_inc(S["wr_in"], 16)
            def store_xn(m):
                for q in range(SPLIT):
                    b = m * SPLIT + q
                    seen(sp, S["xnlo_done"], b + 1)
                    sp.dma_start(xn_dram[bass.ds(b, 1), :, :].rearrange("b p (a n) -> p (b a) n", a=2),
                                 PT[:, :, q * T:(q + 1) * T].bitcast(F32)).then_inc(S[f"xn_stored{q}"], 16)

            store_xn(0)
            with sp.Fori(1, B // SPLIT) as m:
                store_xn(m)

            sp.wait_ge(S["gulo_done"], NP)
            sp.wait_ge(S["xn_stored0"], 16 * B // 2)
            sp.wait_ge(S["xn_stored1"], 16 * B // 2)

            def load_g(n):
                seen(sp, S["t_ready"], 2 * n + 2)
                p = (n + 1) % NP
                sp.dma_start(G_cur[:, :, :, :].rearrange("p a h c -> p (a h c)").bitcast(F32),
                             GU[:, bass.ds(p, 1), 0:512].rearrange("p a n -> p (a n)").bitcast(F32)).then_inc(S["g_loaded"], 16)

            def load_u(n):
                seen(sp, S["out_ready"], 2 * n + 2)
                p = (n + 1) % NP
                sp.dma_start(U_cur[:, :, :, :].rearrange("p a h c -> p (a h c)").bitcast(F32),
                             GU[:, bass.ds(p, 1), 512:1024].rearrange("p a n -> p (a n)").bitcast(F32)).then_inc(S["u_loaded"], 16)

            def load_xn(b):
                seen(sp, S["y_ready"], 2 * NP * b)
                sp.dma_start(xn_cur[:, :, :, :].rearrange("p a t c -> p (a t c)").bitcast(F32),
                             xn_dram[bass.ds(b, 1), :, :].rearrange("b p n -> p (b n)")).then_inc(S["xn_loaded"], 16)

            sp.dma_start(W_ffn[:, :, 0:HID], Wg.rearrange("e c n -> c e n")).then_inc(S["ffn_up_in"], 16)
            sp.dma_start(W_ffn[:, :, HID:2 * HID], Wu.rearrange("e c n -> c e n")).then_inc(S["ffn_up_in"], 16)
            load_g(-1)
            load_u(-1)
            load_xn(0)
            load_g(0)
            load_g(1)
            sp.wait_ge(S["rows_written"], 16)
            sp.dma_start(W_dn[:, :, :, :], Wd.rearrange("e (h p) c -> p e h c", p=P)).then_inc(S["ffn_down_in"], 16)
            with sp.Fori(2, STEPS - 1) as n:
                load_g(n)
                with sp.If((n % NP) == 1):
                    load_xn(n // NP)
                load_u(n - 2)
            load_u(STEPS - 3)
            load_u(STEPS - 2)

            sp.wait_ge(S["table_done"], 1)
            sp.wait_ge(S["rows_written"], 16 * (K * NT * B + 1))

            def load_tile(m, q):
                j = RING * m + q
                row = nc.sync.value_load(table[0:1, 1, bass.ds(j, 1)], min_val=0, max_val=E * REGION - P)
                src = rows_dram[bass.ds(nc.sync.snap(row), P), :]
                seen(sp, S["meta_done"], 2 * (j - RING + 1))
                sp.dma_start(x_in_tile[q], src).then_inc(S[f"x_tile_in{q}"], 16)

            for q in range(RING):
                load_tile(0, q)
            with sp.Fori(1, TURNS) as m:
                for q in range(RING):
                    load_tile(m, q)
            for q in range(LEFT):
                load_tile(TURNS, q)
            for q in range(RING):
                sp.wait_ge(S[f"eo_out{q}"], 16 * (TURNS + (q < LEFT)))
            n = TILES // 4
            for k in range(4):
                for a in range(K):
                    r = a * NTOK + k * n * P
                    sp.dma_start(back[:, a, k * n:(k + 1) * n, :],
                                 expert_dram[r:r + n * P, :].rearrange("(t p) c -> p t c", p=P)).then_inc(back_in[k], 16)
            for k in range(4):
                sp.wait_ge(S["added"], 2 * k + 2)
                sp.dma_start(out[k * n * P:(k + 1) * n * P, :].rearrange("(t p) c -> p t c", p=P),
                             X[:, k * n:(k + 1) * n, :]).then_inc(S["stored"], 16)
            sp.wait_ge(S["stored"], 64)

        @block.gpsimd
        def _(pool):
            nc.gpsimd.memset(ident[:, :], 0.0).then_inc(consts, 1)
            nc.gpsimd.memset(mask[:, :], 0.0).then_inc(consts, 1)
            nc.gpsimd.memset(zero_bf[:, :], 0.0).then_inc(consts, 1)
            nc.gpsimd.memset(power[:, :], -0.5).then_inc(consts, 1)
            nc.gpsimd.memset(eps[:, :], EPS)
            nc.gpsimd.memset(W_dn[:, :, :, :].rearrange("p e h c -> p (e h c)")[:, 0:8 * ROW], 0.0).then_inc(S["zero_tile"], 1)
            pool.wait_ge(consts, 2)
            nc.gpsimd.affine_select(out=ident[:, :], in_=ident[:, :], compare_op=ALU.not_equal, fill=1.0,
                                    base=0, pattern=[[-1, P]], channel_multiplier=1).then_inc(consts, 1)
            nc.gpsimd.affine_select(out=mask[:, T - P:T], in_=mask[:, T - P:T], compare_op=ALU.is_ge, fill=MASKED,
                                    base=0, pattern=[[-1, P]], channel_multiplier=1).then_inc(consts, 1)
            pool.wait_ge(S["zero_tile"], 1)
            n = E * REGION * ROW // P // (8 * ROW)
            nc.gpsimd.dma_start(rows_dram.rearrange("(p a r) c -> p a (r c)", p=P, a=n),
                         W_dn[:, :, :, :].rearrange("p e h c -> p (e h c)")[:, 0:8 * ROW].unsqueeze(1).to_broadcast([P, n, 8 * ROW])
                         ).then_inc(S["rows_written"], 16)
            nc.gpsimd.memset(before_bf[:, :], 0.0).then_inc(consts, 1)
            nc.gpsimd.memset(ones_bf[:, :], 1.0).then_inc(consts, 1)
            pool.wait_ge(consts, 8)
            nc.gpsimd.affine_select(out=before_bf[:, :], in_=before_bf[:, :], compare_op=ALU.is_ge, fill=1.0,
                                    base=0, pattern=[[-1, P]], channel_multiplier=1).then_inc(consts, 1)
            nc.gpsimd.iota(const_i[:, 0:NT * E], pattern=[[0, NT], [1, E]], base=0, channel_multiplier=0).then_inc(consts, 1)
            pool.wait_ge(consts, 10)
            nc.gpsimd.tensor_copy(expert_id[:, :, :].rearrange("p t e -> p (t e)"), const_i[:, 0:NT * E]).then_inc(consts, 1)
            pool.wait_ge(consts, 11)
            nc.gpsimd.iota(const_i[:, 0:SLOTS], pattern=[[1, SLOTS]], base=0, channel_multiplier=0).then_inc(consts, 1)
            pool.wait_ge(consts, 12)
            nc.gpsimd.tensor_copy(slot_id[:, :], const_i[:, 0:SLOTS]).then_inc(consts, 1)
            pool.wait_ge(consts, 13)
            nc.gpsimd.iota(const_i[:, 0:K * NT], pattern=[[NTOK, K], [P, NT]], base=1 - T, channel_multiplier=1).then_inc(consts, 1)
            pool.wait_ge(consts, 14)
            nc.gpsimd.tensor_copy(dest[:, :, :].rearrange("p k t -> p (k t)"), const_i[:, 0:K * NT]).then_inc(consts, 1)
            pool.wait_ge(S["aggr_done"], TILES)
            pool.wait_ge(consts, 6)
            nc.gpsimd.tensor_scalar(rstd[:, :], mv[:, :, 1], EPS, None, ALU.add).then_inc(S["rstd_done"], 1)
            pool.wait_ge(S["rstd_done"], 1)
            nc.gpsimd.tensor_tensor(rstd[:, :], rstd[:, :], power[:, :], ALU.pow).then_inc(S["rstd_done"], 1)

            def norm(n, i):
                seen(pool, S["inv_done"], 2 * (NT * n + i + 1))
                nc.gpsimd.tensor_tensor(p_pair(i), p_pair(i),
                                        row_inv[:, i, :].unsqueeze(2).to_broadcast([P, 2, P * (i + 1)]),
                                        ALU.mult).then_inc(S["norm_pool"], 1)

            def post_rstd(b):
                seen(pool, S["stats2"], 8 * b + 8)
                nc.gpsimd.tensor_tensor(rstd[:, 0:NT], mv[:, 0:NT, 1], eps[:, :], ALU.add).then_inc(S["rstd2"], 1)
                seen(pool, S["rstd2"], 2 * b + 1)
                nc.gpsimd.tensor_tensor(rstd[:, 0:NT], rstd[:, 0:NT], power[:, 0:NT], ALU.pow).then_inc(S["rstd2"], 1)

            def post_scatter(b, first, end):
                if first == 0:
                    seen(pool, S["rows_done"], b + 1)
                    nc.gpsimd.tensor_tensor(gate_p[:, RING:RING + 1], eps[:, 0:1], eps[:, 0:1], ALU.add)
                for k, t in [(k, t) for k in range(K) for t in range(NT)][first:end]:
                    nc.gpsimd.indirect_dma_start(
                        out=rows_dram, out_offset=bass.IndirectOffsetOnAxis(ap=row_i[:, k, t:t + 1], axis=0),
                        in_=routed[:, k, t, :], in_offset=None).then_inc(S["rows_written"], 16)

            pool.wait_ge(S["rows_written"], 16)
            norm(0, 2)
            with pool.Fori(1, NP + 1) as n:
                norm(n - 1, 3)
                norm(n, 2)

            def step(n, k, b):
                if k == 3:
                    post_rstd(b)
                if k in (7, 8):
                    post_scatter(b, 4 * (k - 7), 4 * (k - 7) + 2)
                norm(n - 1, 3)
                if k in (7, 8):
                    post_scatter(b, 4 * (k - 7) + 2, 4 * (k - 7) + 4)
                norm(n, 2)

            with pool.Fori(1, B - 1) as m:
                for k in range(1, NP + 1):
                    step(NP * m + k, k, m - 1)
            for k in range(1, NP - 1):
                step(NP * (B - 1) + k, k, B - 2)
            post_scatter(B - 2, 0, 8)
            norm(STEPS - 2, 3)
            norm(STEPS - 1, 2)
            norm(STEPS - 1, 3)
            post_rstd(B - 1)
            post_scatter(B - 1, 0, 8)

            def scatter_tile(m, q):
                j = RING * m + q
                seen(pool, S["eo_done"], j + 1)
                nc.gpsimd.tensor_tensor(gate_p[:, q:q + 1], eps[:, 0:1], eps[:, 0:1], ALU.add)\
                    .then_inc(S["gated"], 1)
                nc.gpsimd.indirect_dma_start(
                    out=expert_dram, out_offset=bass.IndirectOffsetOnAxis(ap=meta_row[:, q:q + 1], axis=0),
                    in_=eo_sb[q % 2], in_offset=None, bounds_check=K * NTOK - 1, oob_is_err=False).then_inc(S[f"eo_out{q}"], 16)

            for q in range(RING):
                scatter_tile(0, q)
            with pool.Fori(1, TURNS) as m:
                for q in range(RING):
                    scatter_tile(m, q)
            for q in range(LEFT):
                scatter_tile(TURNS, q)

        @block.scalar
        def _(act):
            act.wait_ge(S["wdT_ready"], 1)
            nc.scalar.activation(wdT[:, :], post_ps[:, 0:P], ACT.Copy).then_inc(S["wdT_copied"], 1)
            for g in range(NP):
                act.wait_ge(S["wqT_ready"], g + 1)
                if g:
                    act.wait_ge(S["gu_ready"], g)
                nc.scalar.activation(wqT[:, :], s_ps[0][:, 0:P], ACT.Copy).then_inc(S["wT_copied"], 1)
                nc.scalar.activation(wkT[:, :], s_ps[0][:, P:2 * P], ACT.Copy).then_inc(S["wT_copied"], 1)
                nc.scalar.activation(wvT[:, :], s_ps[0][:, 2 * P:3 * P], ACT.Copy).then_inc(S["wT_copied"], 1)
                act.wait_ge(S["gu_ready"], g + 1)
                for h in range(2):
                    last = nc.scalar.activation(gu_at(g, 0, h), gu_ps[h], ACT.Copy)
                last.then_inc(S["guhi_done"], 1)
            def hi_of_xn(m):
                for q in range(SPLIT):
                    b = m * SPLIT + q
                    seen(act, S["xn_done"], 4 * b + 4)
                    seen(act, S[f"xn_stored{q}"], 16 * m)
                    nc.scalar.activation(PT[:, 0, q * T:(q + 1) * T], xn_f32[:, q, :, :].rearrange("p t c -> p (t c)"),
                                         ACT.Copy).then_inc(S["xnhi_done"], 1)
                    act.wait_ge(S["xT_ready"], b + 1)
                    nc.scalar.activation(XT[:, 0, bass.ds(b * T, T)], xT_ps[q],
                                         ACT.Copy).then_inc(S["xThi_done"], 1)

            hi_of_xn(0)
            with act.Fori(1, B // SPLIT) as m:
                hi_of_xn(m)

            def t_hi(n, h):
                seen(act, S["t_ready"], 2 * n + h + 1)
                seen(act, S["s_ready"], 8 * n)
                nc.scalar.activation(t_sb[:, 0, h, :], t_ps[h][:, :], ACT.Copy).then_inc(S["thi_done"], 1)

            def exps(n, i, h):
                seen(act, S["max_done"], 8 * n + 2 * i + h + 1)
                seen(act, S["inv_done"], 2 * (NT * (n - 1) + i) + h + 1)
                nc.scalar.activation(p_at(i, h), p_at(i, h), ACT.Exp, bias=neg_max[:, i, h:h + 1], scale=-1.0,
                                     accum_out=row_sum[:, i, h:h + 1]).then_inc(S["exp_done"], 1)

            def pt_hi(n, u):
                seen(act, S["pt_ready"], NPT * n + u + 1)
                seen(act, S["y_ready"], 2 * (n - 1) + PARTS[u][0] // 2 + 1)
                nc.scalar.activation(pt_part(u, 0), pt_part(u), ACT.Copy).then_inc(S["pthi_done"], 1)

            def y_hi(n, half):
                seen(act, S["y_ready"], 2 * n + half + 1)
                seen(act, S["out_ready"], 2 * n)
                nc.scalar.activation(y_sb[:, 0, :, half * 256:(half + 1) * 256], y_ps[:, :].rearrange("p (h q) -> p h q", h=2), ACT.Copy)\
                    .then_inc(S["yhi_done"], 1)

            def step(n, cur=True, prev=True, prev2=True, nxt=True, k=None, b=None):
                if prev:
                    pt_hi(n - 1, 0)
                if prev2:
                    y_hi(n - 2, 1)
                if prev:
                    pt_hi(n - 1, 1)
                if cur:
                    exps(n, 0, 0)
                    exps(n, 0, 1)
                if k == 6:
                    post_gap(b)
                if prev:
                    pt_hi(n - 1, 2)
                    pt_hi(n - 1, 3)
                if cur:
                    exps(n, 1, 0)
                    exps(n, 1, 1)
                if prev:
                    pt_hi(n - 1, 4)
                    pt_hi(n - 1, 5)
                if cur:
                    exps(n, 2, 0)
                    exps(n, 2, 1)
                if nxt:
                    t_hi(n + 1, 0)
                if prev:
                    y_hi(n - 1, 0)
                if cur:
                    exps(n, 3, 0)
                if nxt:
                    t_hi(n + 1, 1)
                if cur:
                    exps(n, 3, 1)
                if k == 1:
                    post_out(b)
                if k == 4:
                    post_xn2T(b)

            def post_out(b):
                act.wait_ge(S["out_ready"], 16 * (b + 1))
                nc.scalar.activation(outT[:, :], out_ps[:, :], ACT.Copy).then_inc(S["outT_copied"], 1)

            def post_xn2T(b):
                seen(act, S["xn2T_ready"], b + 1)
                nc.scalar.activation(xn2T[:, :], post_ps[:, :], ACT.Copy).then_inc(S["xn2T_copied"], 1)
                seen(act, S["xn2_done"], 4 * b + 4)
                nc.scalar.activation(routed[:, 1, :, 0:C], routed[:, 0, :, 0:C], ACT.Copy).then_inc(S["rows_copied"], 1)

            def post_gap(b):
                seen(act, S["gap_done"], b + 1)
                nc.scalar.activation(gap_exp[:, :], gap[:, :], ACT.Exp).then_inc(S["gap_exp_done"], 1)

            t_hi(0, 0)
            t_hi(0, 1)
            step(0, prev=False, prev2=False)
            step(1, prev2=False)
            with act.Fori(2, NP + 1) as n:
                step(n)
            with act.Fori(1, B - 1) as m:
                for k in range(1, NP + 1):
                    step(NP * m + k, k=k, b=m - 1)
            for k in range(1, NP - 1):
                step(NP * (B - 1) + k, k=k, b=B - 2)
            step(STEPS - 1, nxt=False)
            step(STEPS, cur=False, nxt=False)
            step(STEPS + 1, cur=False, prev=False, nxt=False)
            post_out(B - 1)
            post_xn2T(B - 1)
            post_gap(B - 1)

            act.wait_ge(S["ffn_up_in"], 32)
            act.wait_ge(S["g_loaded"], 16 * STEPS)
            act.wait_ge(S["u_loaded"], 16 * STEPS)
            for e in range(E):
                nc.scalar.activation(up_hi[:, e, :], W_ffn[:, e, :], ACT.Copy).then_inc(S["up_hi_done"], 1)

            def tile_xT(m, q):
                j = RING * m + q
                seen(act, S["x_tile_T"], j + 1)
                seen(act, S["u_ready"], j - 1)
                nc.scalar.activation(xT_tile[q % 2][:, 0, :], post_ps[:, 0:P], ACT.Copy).then_inc(S["x_hi"], 1)

            def tile_silu(m, q):
                j = RING * m + q
                seen(act, S["g_ready"], j + 1)
                seen(act, S["h_done"], j - 1)
                nc.scalar.activation(silu_sb[q % 2], g_ps[q % 2], ACT.Silu).then_inc(S["silu_done"], 1)

            def tile_hT(m, q):
                j = RING * m + q
                seen(act, S["hT_ready"], j + 1)
                seen(act, S["eo_ready"], j - 1)
                nc.scalar.activation(hT_sb[q % 2][:, :], out_ps[:, :], ACT.Copy).then_inc(S["hT_copied"], 1)

            def turn(m, q, first=False, last=False, drain=False):
                if not last and not drain:
                    tile_xT(*after(m, q))
                if not drain:
                    tile_silu(m, q)
                if not first:
                    tile_hT(*before(m, q))

            tile_xT(0, 0)
            for q in range(RING):
                turn(0, q, first=(q == 0))
            with act.Fori(1, TURNS) as m:
                for q in range(RING):
                    turn(m, q)
            for q in range(LEFT):
                turn(TURNS, q, last=(q == LEFT - 1))
            turn(TURNS, LEFT, drain=True)

        @block.vector
        def _(dve):
            dve.wait_ge(consts, 6)
            for t in range(TILES):
                if t % 8 == 0:
                    dve.wait_ge(x_in[t // 8], 16)
                nc.vector.bn_stats(stats[:, t, :], X[:, t, :]).then_inc(S["stats_done"], 1)
            for t in range(TILES):
                dve.wait_ge(S["stats_done"], t + 1)
                nc.vector.bn_aggr(mv[:, t, :], stats[:, t, :]).then_inc(S["aggr_done"], 1)
            for g in range(NP):
                dve.wait_ge(S["guhi_done"], g + 1)
                for h in range(2):
                    last = nc.vector.tensor_tensor(gu_at(g, 1, h), gu_ps[h], gu_at(g, 0, h).bitcast(F32), ALU.subtract)
                last.then_inc(S["gulo_done"], 1)
            dve.wait_ge(S["rstd_done"], 2)
            def normalise(m):
                for q in range(SPLIT):
                    b = m * SPLIT + q
                    seen(dve, S["xT_ready"], b - 1)
                    seen(dve, S["xnlo_done"], b - 1)
                    for t in range(NT):
                        nc.vector.tensor_scalar(xn_f32[:, q, t, :], X[:, bass.ds(4 * b + t, 1), :].rearrange("p a c -> p (a c)"),
                                                mv[:, bass.ds(4 * b + t, 1), 0], rstd[:, bass.ds(4 * b + t, 1)],
                                                ALU.subtract, ALU.mult).then_inc(S["xn_done"], 1)
                    dve.wait_ge(S["xnhi_done"], b + 1)
                    nc.vector.tensor_tensor(PT[:, 1, q * T:(q + 1) * T], xn_f32[:, q, :, :].rearrange("p t c -> p (t c)"),
                                            PT[:, 0, q * T:(q + 1) * T].bitcast(F32), ALU.subtract).then_inc(S["xnlo_done"], 1)
                    dve.wait_ge(S["xThi_done"], b + 1)
                    nc.vector.tensor_tensor(XT[:, 1, bass.ds(b * T, T)], xT_ps[q],
                                            XT[:, 0, bass.ds(b * T, T)].bitcast(F32), ALU.subtract).then_inc(S["xTlo_done"], 1)

            normalise(0)
            with dve.Fori(1, B // SPLIT) as m:
                normalise(m)

            def t_lo(n, h):
                seen(dve, S["thi_done"], 2 * n + h + 1)
                nc.vector.tensor_tensor(t_sb[:, 1, h, :], t_ps[h][:, :], t_sb[:, 0, h, :].bitcast(F32), ALU.subtract)\
                    .then_inc(S["tlo_done"], 1)

            def maxes(n, i):
                seen(dve, S["pt_ready"], NPT * (n - 1) + parts_to[i])
                w = P * (i + 1)
                for h in range(2):
                    seen(dve, S["s_ready"], 8 * n + 2 * i + h + 1)
                    if i:
                        inv(n, i - 1, h)
                    else:
                        inv(n - 1, NT - 1, h)
                    nc.vector.tensor_tensor_reduce(out=p_at(i, h), in0=s_ps[h][:, 0:w], in1=mask[:, T - w:T],
                                                   scale=-SCALE, scalar=BIG, op0=ALU.add, op1=ALU.min,
                                                   accum_out=neg_max[:, i, h:h + 1]).then_inc(S["max_done"], 1)

            def inv(n, i, h):
                if isinstance(n, int) and n < 0:
                    return
                if i < 2:
                    seen(dve, S["norm_dve"], 2 * (n - 1) + i + 1)
                else:
                    seen(dve, S["norm_pool"], 2 * (n - 1) + i - 2 + 1)
                seen(dve, S["exp_done"], 8 * n + 2 * i + h + 1)
                nc.vector.reciprocal(row_inv[:, i, h:h + 1], row_sum[:, i, h:h + 1]).then_inc(S["inv_done"], 1)

            def norm(n, i):
                seen(dve, S["inv_done"], 2 * (NT * n + i + 1))
                for h in range(2):
                    last = nc.vector.tensor_scalar(p_at(i, h), p_at(i, h), row_inv[:, i, h:h + 1], None, ALU.mult)
                last.then_inc(S["norm_dve"], 1)

            def pt_lo(n, u):
                seen(dve, S["pthi_done"], NPT * n + u + 1)
                nc.vector.tensor_tensor(pt_part(u, 1), pt_part(u), pt_part(u, 0).bitcast(F32), ALU.subtract)\
                    .then_inc(S["ptlo_done"], 1)

            def y_lo(n, half):
                seen(dve, S["yhi_done"], 2 * n + half + 1)
                o = slice(half * 256, (half + 1) * 256)
                nc.vector.tensor_tensor(y_sb[:, 1, :, o], y_ps[:, :].rearrange("p (h q) -> p h q", h=2), y_sb[:, 0, :, o].bitcast(F32), ALU.subtract)\
                    .then_inc(S["ylo_done"], 1)

            def step(n, cur=True, prev=True, prev2=True, nxt=True, k=None, b=None):
                if prev:
                    pt_lo(n - 1, 0)
                if cur:
                    maxes(n, 0)
                elif prev:
                    inv(n - 1, NT - 1, 0)
                    inv(n - 1, NT - 1, 1)
                if prev2:
                    y_lo(n - 2, 1)
                if prev:
                    pt_lo(n - 1, 1)
                if cur:
                    maxes(n, 1)
                if prev:
                    pt_lo(n - 1, 2)
                    pt_lo(n - 1, 3)
                if cur:
                    maxes(n, 2)
                    norm(n, 0)
                if prev:
                    pt_lo(n - 1, 4)
                    pt_lo(n - 1, 5)
                if cur:
                    maxes(n, 3)
                if nxt:
                    t_lo(n + 1, 0)
                if prev:
                    y_lo(n - 1, 0)
                if nxt:
                    t_lo(n + 1, 1)
                if cur:
                    norm(n, 1)
                if k in (2, 3, 5, 6):
                    {2: post_x2, 3: post_xn2, 5: post_choose, 6: post_rows}[k](b)

            def post_x2(b):
                seen(dve, S["outT_ready"], b + 1)
                xs = X[:, bass.ds(4 * b, 4), :].rearrange("p a c -> p (a c)")
                nc.vector.tensor_tensor(xs, post_ps[:, :], xs, ALU.add).then_inc(S["x2_done"], 1)
                seen(dve, S["x2_done"], b + 1)
                nc.vector.tensor_scalar(dest[:, :, :], dest[:, :, :], float(T), None, ALU.add).then_inc(S["dest_done"], 1)
                for t in range(NT):
                    nc.vector.bn_stats(stats[:, t, :], X[:, bass.ds(4 * b + t, 1), :].rearrange("p a c -> p (a c)"))\
                        .then_inc(S["stats2"], 1)
                seen(dve, S["stats2"], 8 * b + 4)
                nc.vector.memset(gate_v[:, :], 0)
                for t in range(NT):
                    nc.vector.bn_aggr(mv[:, t, :], stats[:, t, :]).then_inc(S["stats2"], 1)

            def post_xn2(b):
                seen(dve, S["rstd2"], 2 * b + 2)
                seen(dve, S["rows_written"], 16 * (K * NT * b + 1))
                for t in range(NT):
                    nc.vector.tensor_scalar(routed[:, 0, t, 0:C], X[:, bass.ds(4 * b + t, 1), :].rearrange("p a c -> p (a c)"),
                                            mv[:, t, 0:1], rstd[:, t:t + 1], ALU.subtract, ALU.mult).then_inc(S["xn2_done"], 1)

            ROUTING = 21

            def post_choose(b):
                def made(k):
                    seen(dve, S["routing"], ROUTING * b + k)

                def sig(ins):
                    ins.then_inc(S["routing"], 1)

                seen(dve, S["logits_ready"], b + 1)
                sig(nc.vector.tensor_copy(logit[:, :, :].rearrange("p t e -> p (t e)"), post_ps[:, 0:NT * E]))
                for t in range(NT):
                    sig(nc.vector.max(top[:, t, :], post_ps[:, t * E:(t + 1) * E]))
                made(5)
                nc.vector.tensor_tensor(gap[:, :], top[:, :, 1], top[:, :, 0], ALU.subtract).then_inc(S["gap_done"], 1)
                for t in range(NT):
                    sig(nc.vector.max_index(top_i[:, t, :], top[:, t, :], logit[:, t, :]))
                made(9)
                sig(nc.vector.tensor_copy(top_f[:, :, :], top_i[:, :, 0:K]))
                made(10)
                for k in range(K):
                    sig(nc.vector.tensor_tensor(chosen[:, k, :, :], expert_id[:, :, :],
                                                top_f[:, :, k].unsqueeze(2).to_broadcast([P, NT, E]), ALU.is_equal))
                made(12)
                nc.vector.tensor_tensor(chosen_bf[:, :, :], chosen[:, 0, :, :], chosen[:, 1, :, :], ALU.add)\
                    .then_inc(S["chosen_done"], 1)

            def post_rows(b):
                def made(k):
                    seen(dve, S["routing"], ROUTING * b + k)

                def sig(ins):
                    ins.then_inc(S["routing"], 1)

                seen(dve, S["ranks_ready"], b + 1)
                sig(nc.vector.tensor_tensor(pos[:, :, :], post_ps[:, RANK_COL:RANK_COL + NT * E].rearrange("p (t e) -> p t e", e=E),
                                            base[:, :].unsqueeze(1).to_broadcast([P, NT, E]), ALU.add))
                made(13)
                sig(nc.vector.tensor_tensor(base[:, :], post_ps[:, TOTAL_COL:TOTAL_COL + E], base[:, :], ALU.add))
                for k in range(K):
                    sig(nc.vector.tensor_tensor(picked[:, k, :, :], chosen[:, k, :, :], pos[:, :, :], ALU.mult))
                made(16)
                sig(nc.vector.tensor_reduce(row_f[:, :, :], picked[:, :, :, :], AX.X, ALU.add))
                seen(dve, S["gap_exp_done"], b + 1)
                sig(nc.vector.tensor_scalar(weight[:, 1, :], gap_exp[:, :], 1.0, None, ALU.add))
                made(18)
                sig(nc.vector.reciprocal(weight[:, 0, :], weight[:, 1, :]))
                sig(nc.vector.tensor_copy(row_i[:, :, :], row_f[:, :, :]))
                made(19)
                sig(nc.vector.tensor_tensor(weight[:, 1, :], gap_exp[:, :], weight[:, 0, :], ALU.mult))
                made(21)
                nc.vector.tensor_scalar(routed[:, :, :, C], weight[:, :, :], DEPTH_SCALE, None, ALU.mult)
                seen(dve, S["rows_copied"], b + 1)
                seen(dve, S["dest_done"], b + 1)
                nc.vector.tensor_copy(routed[:, :, :, C + 1], dest[:, :, :]).then_inc(S["rows_done"], 1)

            nc.vector.tensor_scalar(base[:, :], expert_id[:, 0, :], float(REGION), None, ALU.mult).then_inc(S["base_set"], 1)
            dve.wait_ge(S["base_set"], 1)
            t_lo(0, 0)
            t_lo(0, 1)
            step(0, prev=False, prev2=False)
            step(1, prev2=False)
            with dve.Fori(2, NP + 1) as n:
                step(n)
            with dve.Fori(1, B - 1) as m:
                for k in range(1, NP + 1):
                    step(NP * m + k, k=k, b=m - 1)
            for k in range(1, NP - 1):
                step(NP * (B - 1) + k, k=k, b=B - 2)
            step(STEPS - 1, nxt=False)
            step(STEPS, cur=False, nxt=False)
            step(STEPS + 1, cur=False, prev=False, nxt=False)
            post_x2(B - 1)
            post_xn2(B - 1)
            post_choose(B - 1)
            post_rows(B - 1)

            tabled = [0]

            def tab(ins):
                tabled[0] += 1
                ins.then_inc(S["tabling"], 1)
                dve.wait_ge(S["tabling"], tabled[0])

            tab(nc.vector.scalar_tensor_tensor(count[:, :], expert_id[0:1, 0, :], float(-REGION), base[0:1, :], ALU.mult, ALU.add))
            tab(nc.vector.tensor_scalar(count_i[:, :], count[:, :], float(P - 1), None, ALU.add))
            tab(nc.vector.tensor_single_scalar(count_i[:, :], count_i[:, :], 7, op=ALU.arith_shift_right))
            tab(nc.vector.tensor_copy(tiles_of[:, :], count_i[:, :]))
            tab(nc.vector.tensor_copy(ends[:, :], tiles_of[:, :]))
            for e in range(1, E):
                tab(nc.vector.tensor_tensor(ends[:, e:e + 1], ends[:, e - 1:e], ends[:, e:e + 1], ALU.add))
            tab(nc.vector.tensor_scalar(jump[:, :], tiles_of[:, :], float(-P), float(REGION), ALU.mult, ALU.add))
            shape = [1, SLOTS, E - 1]
            tab(nc.vector.tensor_tensor(past[:, :, :], slot_id[0:1, :].unsqueeze(2).to_broadcast(shape),
                                        ends[:, 0:E - 1].unsqueeze(1).to_broadcast(shape), ALU.is_ge))
            tab(nc.vector.tensor_tensor(jumps[:, :, :], past[:, :, :], jump[:, 0:E - 1].unsqueeze(1).to_broadcast(shape), ALU.mult))
            tab(nc.vector.tensor_reduce(table_f[:, 0, :], past[:, :, :], AX.X, ALU.add))
            tab(nc.vector.tensor_reduce(table_f[:, 1, :], jumps[:, :, :], AX.X, ALU.add))
            tab(nc.vector.scalar_tensor_tensor(table_f[:, 1, :], slot_id[0:1, :], float(P), table_f[:, 1, :], ALU.mult, ALU.add))
            tab(nc.vector.tensor_scalar(table_f[:, 1, :], table_f[:, 1, :], float(E * REGION - P), None, ALU.min))
            nc.vector.tensor_copy(table[:, :, :], table_f[:, :, :]).then_inc(S["table_done"], 1)

            dve.wait_ge(S["s_ready"], 8 * STEPS)
            for e in range(E):
                dve.wait_ge(S["up_hi_done"], e + 1)
                nc.vector.tensor_tensor(up_lo[:, e, :], W_ffn[:, e, :], up_hi[:, e, :].bitcast(F32), ALU.subtract)\
                    .then_inc(S["up_lo_done"], 1)

            def tile_xT(m, q):
                j = RING * m + q
                seen(dve, S["x_hi"], j + 1)
                nc.vector.tensor_tensor(xT_tile[q % 2][:, 1, :], post_ps[:, 0:P], xT_tile[q % 2][:, 0, :].bitcast(F32), ALU.subtract)\
                    .then_inc(S["x_lo"], 1)

            def tile_meta(m, q):
                j = RING * m + q
                seen(dve, S[f"x_tile_in{q}"], 16 * (m + 1))
                seen(dve, S["gated"], j - RING + 1)
                seen(dve, S[f"eo_out{q}"], 16 * m)
                nc.vector.tensor_copy(meta_w[:, q:q + 1], x_in_tile[q][:, C:C + 1]).then_inc(S["meta_done"], 1)
                nc.vector.tensor_scalar(meta_row[:, q:q + 1], x_in_tile[q][:, C + 1:C + 2], -1.0, None, ALU.add)\
                    .then_inc(S["meta_done"], 1)

            def tile_h(m, q):
                j = RING * m + q
                seen(dve, S["silu_done"], j + 1)
                seen(dve, S["u_ready"], j + 1)
                seen(dve, S["hT_ready"], j - 1)
                nc.vector.tensor_tensor(h_sb[q % 2], u_ps[q % 2], silu_sb[q % 2], ALU.mult).then_inc(S["h_done"], 1)

            def tile_eo(m, q):
                j = RING * m + q
                seen(dve, S["eo_ready"], j + 1)
                seen(dve, S["meta_done"], 2 * (j + 1))
                seen(dve, S[f"eo_out{(q - 2) % RING}"], 16 * (m + 1) if q >= 2 else 16 * m)
                nc.vector.tensor_scalar(eo_sb[q % 2], eo_ps[q % 2], meta_w[:, q:q + 1], None, ALU.mult).then_inc(S["eo_done"], 1)

            def turn(m, q, first=False, last=False, drain=False):
                if not last and not drain:
                    tile_xT(*after(m, q))
                    tile_meta(*after(m, q))
                if not drain:
                    tile_h(m, q)
                if not first:
                    tile_eo(*before(m, q))

            tile_xT(0, 0)
            tile_meta(0, 0)
            for q in range(RING):
                turn(0, q, first=(q == 0))
            with dve.Fori(1, TURNS) as m:
                for q in range(RING):
                    turn(m, q)
            for q in range(LEFT):
                turn(TURNS, q, last=(q == LEFT - 1))
            turn(TURNS, LEFT, drain=True)

            n = TILES // 4
            for k in range(4):
                xs = X[:, k * n:(k + 1) * n, :]
                dve.wait_ge(back_in[k], 32)
                nc.vector.tensor_tensor(xs, back[:, 0, k * n:(k + 1) * n, :], xs, ALU.add).then_inc(S["added"], 1)
                dve.wait_ge(S["added"], 2 * k + 1)
                nc.vector.tensor_tensor(xs, back[:, 1, k * n:(k + 1) * n, :], xs, ALU.add).then_inc(S["added"], 1)

        @block.tensor
        def _(pe):
            pe.wait_ge(consts, 6)
            pe.wait_ge(w_in, 64)
            nc.tensor.transpose(post_ps[:, 0:P], w_down_sb, ident[:, :]).then_inc(S["wdT_ready"], 1)
            pe.wait_ge(S["wdT_copied"], 1)
            for g in range(NP):
                d = slice(g * P, (g + 1) * P)
                if g:
                    pe.wait_ge(S["wT_copied"], 3 * g)
                nc.tensor.transpose(s_ps[0][:, 0:P], w_q_sb[:, d], ident[:, :])
                nc.tensor.matmul(s_ps[0][:, P:2 * P], w_up_sb[:, g * P:(g + 1) * P], wdT[:, :], start=True, stop=True)
                nc.tensor.matmul(s_ps[0][:, 2 * P:3 * P], w_up_sb[:, NH * HD + g * P:NH * HD + (g + 1) * P], wdT[:, :],
                                 start=True, stop=True).then_inc(S["wqT_ready"], 1)
                pe.wait_ge(S["wT_copied"], 3 * g + 3)
                if g:
                    pe.wait_ge(S["gulo_done"], g)
                for h in range(2):
                    k = slice(h * HD, (h + 1) * HD)
                    nc.tensor.matmul(gu_ps[h][:, 0, :], wqT[k, :], wkT[k, :], start=True, stop=True)
                    last = nc.tensor.matmul(gu_ps[h][:, 1, :], wvT[k, :], w_out_sb[k, g, :], start=True, stop=True)
                last.then_inc(S["gu_ready"], 1)
            def transpose_xn(m):
                for q in range(SPLIT):
                    b = m * SPLIT + q
                    pe.wait_ge(S["xn_done"], 4 * b + 4)
                    seen(pe, S["xTlo_done"], b - 1)
                    for t in range(NT):
                        last = nc.tensor.transpose(xT_ps[q][:, t * P:(t + 1) * P], xn_f32[:, q, t, :], ident[:, :])
                    last.then_inc(S["xT_ready"], 1)

            transpose_xn(0)
            with pe.Fori(1, B // SPLIT) as m:
                transpose_xn(m)

            def passes(dst, ws, vs, start, stop, **kw):
                nc.tensor.matmul(dst, ws[0], vs[0], start=start, stop=False, **kw)
                nc.tensor.matmul(dst, ws[1], vs[0], start=False, stop=False, **kw)
                return nc.tensor.matmul(dst, ws[0], vs[1], start=False, stop=stop, **kw)

            def xT_at(part, b, w):
                return XT[:, part, bass.ds(b * T, w)]

            def project(n, h, b):
                seen(pe, S["g_loaded"], 16 * (n + 1))
                seen(pe, S["ptlo_done"], NPT * (n - 2) + (3 if h == 0 else 5))
                passes(t_ps[h][:, :], [G_cur[:, a, h, :] for a in range(2)], [xT_at(a, b, T) for a in range(2)],
                       True, True).then_inc(S["t_ready"], 1)

            def scores(n, i, b):
                w = max(256, P * (i + 1))
                for h in range(2):
                    if i == 0:
                        seen(pe, S["tlo_done"], 2 * n + h + 1)
                    seen(pe, S["max_done"], 8 * n + 2 * i + h - 1)
                    passes(s_ps[h][:, 0:w], [t_sb[:, a, h, i * P:(i + 1) * P] for a in range(2)],
                           [xT_at(a, b, w) for a in range(2)], True, True).then_inc(S["s_ready"], 1)

            def transposes(n, i):
                if i < 2:
                    seen(pe, S["norm_dve"], 2 * n + i + 1)
                else:
                    seen(pe, S["norm_pool"], 2 * n + i - 2 + 1)
                for u in range(parts_to[i - 1] if i else 0, parts_to[i]):
                    name, count = [("tlo_done", 2 * n + 3), ("ptlo_done", NPT * n), ("ptlo_done", NPT * n + 1),
                                   ("ylo_done", 2 * n), ("tlo_done", 2 * n + 4), ("ptlo_done", NPT * n + 2)][u]
                    seen(pe, S[name], min(count, 2 * STEPS) if isinstance(n, int) and name == "tlo_done" else count)
                    dst, h = pt_part(u), PARTS[u][1]
                    for g in range(2) if h is None else [h]:
                        for j in range(i + 1):
                            last = nc.tensor.transpose(dst[:, g, j, :] if h is None else dst[:, j, :],
                                                       p_at(i, g)[:, j * P:(j + 1) * P], ident[:, :])
                    last.then_inc(S["pt_ready"], 1)

            def values(n, half, b):
                seen(pe, S["ptlo_done"], NPT * n + (4 if half == 0 else 6))
                seen(pe, S["ylo_done"], 2 * n + half)
                seen(pe, S["xn_loaded"], 16 * (b + 1))
                keys = 2 * half + 2
                for j in range(keys):
                    if j < keys - 1:
                        dst = y_ps[:, :]
                        src = [pt_at(a, half)[:, j, :, :, :].rearrange("p h i q -> p (h i q)") for a in range(2)]
                    else:
                        dst = y_ps[:, :].rearrange("p (h q) -> p h q", h=2)[:, :, P:256]
                        src = [pt_at(a, half)[:, j, :, 1, :] for a in range(2)]
                    last = passes(dst, [xn_cur[:, a, j, :] for a in range(2)], src, j == 0, j == keys - 1)
                last.then_inc(S["y_ready"], 1)

            def project_out(n, h):
                if h == 0:
                    seen(pe, S["u_loaded"], 16 * (n + 1))
                    seen(pe, S["ylo_done"], 2 * n + 2)
                passes(out_ps[:, :], [U_cur[:, a, h, :] for a in range(2)], [y_sb[:, a, h, :] for a in range(2)],
                       False, True, skip_group_check=True).then_inc(S["out_ready"], 1)

            def clear_out():
                nc.tensor.matmul(out_ps[:, :], zero_bf[:, 0:P], zero_bf[:, :], start=True, stop=True)

            def step(m, k, cur=True, prev=True, prev2=True, nxt=True, b=None):
                n = NP * m + k
                if prev:
                    transposes(n - 1, 0)
                if prev2:
                    values(n - 2, 1, m + (k - 2) // NP)
                if cur:
                    scores(n, 0, m + k // NP)
                if prev:
                    transposes(n - 1, 1)
                if cur:
                    scores(n, 1, m + k // NP)
                if b is not None and k in (2, 4, 5, 6):
                    {2: post_out, 4: post_xn2T, 5: post_logits, 6: post_ranks}[k](b)
                if prev2:
                    project_out(n - 2, 0)
                if prev:
                    transposes(n - 1, 2)
                if cur:
                    scores(n, 2, m + k // NP)
                if prev2:
                    project_out(n - 2, 1)
                if prev:
                    transposes(n - 1, 3)
                if cur:
                    scores(n, 3, m + k // NP)
                if nxt:
                    project(n + 1, 0, m + (k + 1) // NP)
                if prev:
                    values(n - 1, 0, m + (k - 1) // NP)
                if nxt:
                    project(n + 1, 1, m + (k + 1) // NP)

            def post_out(b, clear=True):
                pe.wait_ge(S["outT_copied"], b + 1)
                if clear:
                    clear_out()
                for t in range(NT):
                    last = nc.tensor.transpose(post_ps[:, t * P:(t + 1) * P], outT[:, t * P:(t + 1) * P], ident[:, :])
                last.then_inc(S["outT_ready"], 1)

            def post_xn2T(b):
                seen(pe, S["xn2_done"], 4 * b + 4)
                seen(pe, S["x2_done"], b + 1)
                for t in range(NT):
                    last = nc.tensor.transpose(post_ps[:, t * P:(t + 1) * P], routed[:, 0, t, 0:C], ident[:, :])
                last.then_inc(S["xn2T_ready"], 1)

            def post_logits(b):
                pe.wait_ge(S["wr_in"], 16)
                seen(pe, S["xn2T_copied"], b + 1)
                for t in range(NT):
                    last = nc.tensor.matmul(post_ps[:, t * E:(t + 1) * E], xn2T[:, t * P:(t + 1) * P], Wr_sb[:, :],
                                            start=True, stop=True)
                last.then_inc(S["logits_ready"], 1)

            def post_ranks(b):
                seen(pe, S["chosen_done"], b + 1)
                ranks = post_ps[:, RANK_COL:RANK_COL + NT * E].rearrange("p (t e) -> p t e", e=E)
                total = post_ps[:, TOTAL_COL:TOTAL_COL + E]
                kw = dict(skip_group_check=True)
                nc.tensor.matmul(ranks, before_bf[:, :], chosen_bf[:, :, :], start=True, stop=True, **kw)
                for t in range(NT - 1):
                    nc.tensor.matmul(ranks[:, t + 1:NT, :], ones_bf[:, :],
                                     chosen_bf[:, t:t + 1, :].to_broadcast([P, NT - 1 - t, E]), start=False, stop=True, **kw)
                for t in range(NT):
                    last = nc.tensor.matmul(total, ones_bf[:, :], chosen_bf[:, t, :], start=False, stop=True, **kw)
                last.then_inc(S["ranks_ready"], 1)

            pe.wait_ge(S["xTlo_done"], B)
            clear_out()
            project(0, 0, 0)
            project(0, 1, 0)
            step(0, 0, prev=False, prev2=False)
            step(0, 1, prev2=False)
            with pe.Fori(2, NP + 1) as k:
                step(0, k)
            with pe.Fori(1, B - 1) as m:
                for k in range(1, NP + 1):
                    step(m, k, b=m - 1)
            for k in range(1, NP - 1):
                step(B - 1, k, b=B - 2)
            step(B - 1, NP - 1, nxt=False)
            step(B - 1, NP, cur=False, nxt=False)
            step(B - 1, NP + 1, cur=False, prev=False, nxt=False)
            post_out(B - 1, clear=False)
            post_xn2T(B - 1)
            post_logits(B - 1)
            post_ranks(B - 1)

            def tile_xT(m, q):
                j = RING * m + q
                seen(pe, S[f"x_tile_in{q}"], 16 * (m + 1))
                seen(pe, S["x_lo"], j)
                nc.tensor.transpose(post_ps[:, 0:P], x_in_tile[q][:, 0:C], ident[:, :]).then_inc(S["x_tile_T"], 1)

            def tile_up(j, q, e, half):
                dst, o = (g_ps[q % 2], 0) if half == 0 else (u_ps[q % 2], HID)
                return passes(dst, [xT_tile[q % 2][:, a, :] for a in range(2)],
                              [w[:, bass.ds(e, 1), o:o + HID].rearrange("p a n -> p (a n)") for w in (up_hi, up_lo)], True, True)

            def tile_g(m, q, e):
                j = RING * m + q
                seen(pe, S["x_lo"], j + 1)
                seen(pe, S["h_done"], j - 1)
                tile_up(j, q, e, 0).then_inc(S["g_ready"], 1)

            def tile_u(m, q, e):
                tile_up(2 * m + q, q, e, 1).then_inc(S["u_ready"], 1)

            def tile_hT(m, q):
                j = RING * m + q
                seen(pe, S["h_done"], j + 1)
                seen(pe, S["hT_copied"], j)
                for k in range(HC):
                    last = nc.tensor.transpose(out_ps[:, k * P:(k + 1) * P], h_sb[q % 2][:, k * P:(k + 1) * P], ident[:, :])
                last.then_inc(S["hT_ready"], 1)

            def tile_down(m, q, e):
                j = RING * m + q
                seen(pe, S["hT_copied"], j + 1)
                seen(pe, S["eo_done"], j - 1)
                for k in range(HC):
                    last = nc.tensor.matmul(eo_ps[q % 2], hT_sb[q % 2][:, k * P:(k + 1) * P],
                                            W_dn[:, bass.ds(e, 1), k, :].rearrange("p a c -> p (a c)"),
                                            start=(k == 0), stop=(k == HC - 1))
                last.then_inc(S["eo_ready"], 1)

            expert_reg = [nc.tensor.alloc_register(f"expert{q}") for q in range(RING)]

            def load_expert(m, q):
                nc.tensor.reg_load(expert_reg[q], table[0:1, 0, bass.ds(RING * m + q, 1)])

            def expert(q):
                return nc.tensor.snap(expert_reg[q], min_val=0, max_val=E - 1)

            def turn(m, q, first=False, last=False, drain=False):
                if not last and not drain:
                    tile_xT(*after(m, q))
                if not drain:
                    e = expert(q)
                    tile_g(m, q, e)
                if not first:
                    tile_hT(*before(m, q))
                if not drain:
                    tile_u(m, q, e)
                if not last and not drain:
                    load_expert(*after(m, q))
                if not first:
                    tile_down(*before(m, q), expert((q - 1) % RING))

            pe.wait_ge(S["table_done"], 1)
            pe.wait_ge(S["up_lo_done"], E)
            pe.wait_ge(S["ffn_down_in"], 16)
            load_expert(0, 0)
            tile_xT(0, 0)
            for q in range(RING):
                turn(0, q, first=(q == 0))
            with pe.Fori(1, TURNS) as m:
                for q in range(RING):
                    turn(m, q)
            for q in range(LEFT):
                turn(TURNS, q, last=(q == LEFT - 1))
            turn(TURNS, LEFT, drain=True)


_INS = {"L0_attn_x": (NTOK, C), "L0_attn_w_kv_down": None, "L0_attn_w_kv_up": None, "L0_attn_w_q": None,
        "L0_attn_w_out": None, "L0_ffn_Wr": None, "L0_ffn_Wg": None, "L0_ffn_Wu": None, "L0_ffn_Wd": None}


def kernel(**inputs):
    import concourse.bacc as bacc
    from concourse.bass_utils import run_bass_kernel_spmd

    nc = bacc.Bacc("TRN2", target_bir_lowering=False, num_devices=1)
    arrays, args = {}, []
    for name, shape in _INS.items():
        a = np.ascontiguousarray(inputs[name])
        a = a.reshape(shape) if shape else a
        arrays[f"in_{name}"] = a
        args.append(nc.dram_tensor(f"in_{name}", a.shape, mybir.dt.from_np(a.dtype), kind="ExternalInput").ap())
    args.append(nc.dram_tensor("out_0", (NTOK, C), F32, kind="ExternalOutput").ap())
    layer(nc, *args)
    r = run_bass_kernel_spmd(nc, [arrays], core_ids=[0])
    return r.results[0]["out_0"].reshape(B, T, C)
```

```python
from contextlib import ExitStack

import numpy as np
import concourse.bass as bass
from concourse import mybir

F32 = mybir.dt.float32
F32R = mybir.dt.float32r
BF16 = mybir.dt.bfloat16
I32 = mybir.dt.int32
U32 = mybir.dt.uint32
ALU = mybir.AluOpType
ACT = mybir.ActivationFunctionType
AX = mybir.AxisListType

P = 128
B, T, C = 8, 512, 128
NT = T // P
NH, HD = 16, 64
NP = NH // 2
R = 128
NTOK = B * T
TILES = NTOK // P
RING = 4
E, HID, K = 8, 512, 2
HC = HID // P
STEPS = B * NP
REGION = NTOK
XB = 4
FILLS = NP
ROW = C + 2
SLOTS = (NTOK * K + E * (P - 1)) // P
TURNS, LEFT = divmod(SLOTS, RING)
SCALE = HD ** -0.5
DEPTH_SCALE = 12 ** -0.5
EPS = 1e-5
MASKED = -1e30
BIG = 3e38
RANK_COL, TOTAL_COL = 64, 128


def seen(eng, sem, count):
    if not isinstance(count, int) or count > 0:
        eng.wait_ge(sem, count)


def before(m, q):
    return (m, q - 1) if q else (m - 1, RING - 1)


def after(m, q):
    return (m, q + 1) if q < RING - 1 else (m + 1, 0)


def layer(nc, x, w_down, w_up, w_q, w_out, Wr, Wg, Wu, Wd, out):
    ctx = ExitStack()
    with ctx:
        def sb(name, shape, dt=F32):
            return ctx.enter_context(nc.sbuf_tensor(name, shape, dt))

        def sem(name):
            return ctx.enter_context(nc.semaphore(name))

        xn_dram = nc.dram_tensor("xn_scratch", [B, P, 2 * T], F32).ap()
        rows_dram = nc.dram_tensor("routed_rows", [E * REGION, ROW], F32).ap()
        expert_dram = nc.dram_tensor("expert_out", [K * NTOK, C], F32).ap()

        X = sb("X", [P, TILES, C])
        XT = sb("XT", [P, 2, NTOK], F32R)
        GU = sb("GU", [P, NP, 1024], F32R)
        W_ffn = sb("W_ffn", [P, E, 2 * HID])
        W_dn = sb("W_dn", [P, E, HC, C])
        prob = sb("prob", [P, 2 * 1280])
        PT = sb("PT", [P, 2, 3072], F32R)
        t_sb = sb("t_sb", [P, 2, 2, T], F32R)
        y_sb = sb("y_sb", [P, 2, 2, T], F32R)
        G_cur = sb("G_cur", [P, 2, 2, P], F32R)
        U_cur = sb("U_cur", [P, 2, 2, P], F32R)
        xn_cur = sb("xn_cur", [P, 2, NT, C], F32R)
        mask = sb("mask", [P, T])
        ident = sb("ident", [P, P])
        zero_bf = sb("zero_bf", [P, T], BF16)
        wdT = sb("wdT", [P, P])
        row_sum = sb("row_sum", [P, NT, 2])
        row_inv = sb("row_inv", [P, NT, 2])
        neg_max = sb("neg_max", [P, NT, 2])
        stats = sb("stats", [P, TILES, 6])
        mv = sb("mv", [P, TILES, 2])
        rstd = sb("rstd", [P, TILES])
        power = sb("power", [P, TILES])
        eps = sb("eps", [P, NT])
        outT = sb("outT", [P, T])
        Wr_sb = sb("Wr_sb", [P, E])
        routed = sb("routed", [P, K, NT, ROW])
        xn2T = sb("xn2T", [P, T])
        before_bf = sb("before_bf", [P, P], BF16)
        ones_bf = sb("ones_bf", [P, P], BF16)
        const_i = sb("const_i", [P, P], I32)
        expert_id = sb("expert_id", [P, NT, E])
        slot_id = sb("slot_id", [P, SLOTS])
        dest = sb("dest", [P, K, NT])
        logit = sb("logit", [P, NT, E])
        top = sb("top", [P, NT, 8])
        top_i = sb("top_i", [P, NT, 8], U32)
        top_f = sb("top_f", [P, NT, K])
        chosen = sb("chosen", [P, K, NT, E])
        chosen_bf = sb("chosen_bf", [P, NT, E], BF16)
        gap = sb("gap", [P, NT])
        gap_exp = sb("gap_exp", [P, NT])
        weight = sb("weight", [P, K, NT])
        base = sb("base", [P, E])
        pos = sb("pos", [P, NT, E])
        picked = sb("picked", [P, K, NT, E])
        row_f = sb("row_f", [P, K, NT])
        row_i = sb("row_i", [P, K, NT], I32)
        count = sb("count", [1, E])
        count_i = sb("count_i", [1, E], I32)
        tiles_of = sb("tiles_of", [1, E])
        ends = sb("ends", [1, E])
        jump = sb("jump", [1, E])
        past, jumps = (prob[0:1, o:o + SLOTS * (E - 1)].rearrange("p (j e) -> p j e", e=E - 1) for o in (0, T))
        table_f = sb("table_f", [1, 2, SLOTS])
        table = sb("table", [1, 2, SLOTS], I32)
        gate_v = sb("gate_v", [P, 1], I32)
        gate_p = sb("gate_p", [P, RING + 1])
        meta_w = sb("meta_w", [P, RING])
        meta_row = sb("meta_row", [P, RING], I32)
        up_hi = GU[:, :, :]
        up_lo = XT[:, :, :].rearrange("p a n -> p (a n)").rearrange("p (e n) -> p e n", e=E)
        x_in_tile = [routed[:, 0, q, :] for q in range(RING)]
        xT_tile = [t_sb[:, q, :, 0:P] for q in range(2)]
        silu_sb = [prob[:, q * T:(q + 1) * T] for q in range(2)]
        h_sb = [prob[:, (2 + q) * T:(3 + q) * T] for q in range(2)]
        hT_sb = [outT, xn2T]
        eo_sb = [prob[:, 4 * T + q * C:4 * T + (q + 1) * C] for q in range(2)]
        back = W_ffn[:, :, :].rearrange("p e n -> p (e n)").rearrange("p (k t c) -> p k t c", k=K, c=C)

        w_up_sb = W_ffn[:, 0:2, :].rearrange("p a n -> p (a n)")
        w_q_sb = W_ffn[:, 2, :]
        w_out_sb = W_ffn[:, 3, :].rearrange("p (g c) -> p g c", g=NP)
        w_down_sb = W_ffn[:, 4, 0:R]
        xn_f32 = prob[:, 0:2 * T].rearrange("p (q t c) -> p q t c", q=2, c=C)

        s_ps = [ctx.enter_context(nc.psum_tensor(f"s_ps{h}", [P, T], F32)) for h in range(2)]
        bank_a, bank_b, bank_c, bank_d = (ctx.enter_context(nc.psum_tensor(f"bank_{k}", [P, T], F32)) for k in "abcd")
        pt_ps = [bank_d, bank_c, bank_a, bank_b, bank_c, bank_d]
        t_ps = [bank_b, bank_a]
        y_ps = [bank_c, bank_b]
        out_ps = ctx.enter_context(nc.psum_tensor("out_ps", [P, T], F32))
        post_ps = ctx.enter_context(nc.psum_tensor("post_ps", [P, T], F32))

        gu_ps = [[ps[:, 0:256].rearrange("p (k c) -> p k c", k=2) for ps in pair] for pair in ((s_ps[1], bank_d), (bank_c, out_ps))]
        wT = [prob[:, 2 * T + q * 3 * P:2 * T + (q + 1) * 3 * P] for q in range(2)]

        SPLIT_HI, SPLIT_LO = [0, 1, 2, 3, 4, 5, 6, 7], [0, 1, 2, 4, 5, 6, 3, 7]
        HI_AT = {k: k - 1 for k in range(2, NP + 2)}
        LO_AT = {2: 1, 3: 2, 4: 3, 5: 3, 6: 4, 7: 5, 8: 6, 9: 8}

        g_ps = [s_ps[0][:, :], bank_d[:, :]]
        u_ps = [s_ps[1][:, :], bank_c[:, :]]
        eo_ps = [bank_a[:, 0:P], bank_b[:, 0:P]]

        xT_ps = [bank_a[:, :], bank_b[:, :]]

        PARTS = [(0, None), (1, None), (2, 0), (2, 1), (3, 0), (3, 1)]
        NPT = len(PARTS)
        parts_to = [1, 2, 4, 6]

        def gu_at(g, part, h):
            return GU[:, g, :].rearrange("p (k a h c) -> p k a h c", k=2, a=2, h=2)[:, :, part, h, :]

        def p_pair(i):
            o = P * i * (i + 1)
            return prob[:, o:o + 2 * P * (i + 1)].rearrange("p (h k) -> p h k", h=2)

        def p_at(i, h):
            o = 128 * i * (i + 1) + h * 128 * (i + 1)
            return prob[:, o:o + 128 * (i + 1)]

        def pt_at(part, half):
            v = PT[:, part, 0:1024] if half == 0 else PT[:, part, 1024:3072]
            return v.rearrange("p (j h i q) -> p j h i q", h=2, i=2, q=P)

        def pt_part(u, part=None):
            i, h = PARTS[u]
            if part is None:
                v = pt_ps[u][:, 0:(i + 1) * P * (2 if h is None else 1)]
                return v.rearrange("p (h j q) -> p h j q", h=2, q=P) if h is None else v.rearrange("p (j q) -> p j q", q=P)
            v = pt_at(part, i // 2)[:, 0:i + 1, :, i % 2, :]
            return v.rearrange("p j h q -> p h j q") if h is None else v[:, :, h, :]

        x_in = [sem(f"x_in{k}") for k in range(4)]
        w_in = sem("w_in")
        consts = sem("consts")
        S = {n: sem(n) for n in (
            "stats_done", "aggr_done", "rstd_done", "xn_done", "xnhi_done", "xnlo_done", "xT_ready", "xThi_done", "xTlo_done",
            "wdT_ready", "wdT_copied", "wT_ready", "wT_copied", "gu_ready", "guhi_done", "gulo_done",
            "g_loaded", "u_loaded", "xn_loaded",
            "t_ready", "thi_done", "tlo_done", "s_ready", "max_done", "exp_done", "inv_done", "norm_done",
            "pt_ready", "pthi_done", "ptlo_done", "y_ready", "yhi_done", "ylo_done", "out_ready",
            "outT_copied", "outT_ready", "x2_done", "stats2", "rstd2", "xn2_done", "xn2T_ready", "xn2T_copied", "rows_copied",
            "logits_ready", "routing", "chosen_done", "gap_done", "gap_exp_done", "ranks_ready", "rows_done", "rows_written", "dest_done", "base_set", "gated",
            "wr_in", "zero_tile", "ffn_up_in", "ffn_down_in", "table_done", "tabling", "split_hi", "split_lo",
            "x_tile_in0", "x_tile_in1", "x_tile_in2", "x_tile_in3", "x_tile_T", "x_hi", "x_lo", "meta_done", "g_ready", "u_ready", "silu_done", "h_done",
            "hT_ready", "hT_copied", "eo_ready", "eo_done", "eo_out0", "eo_out1", "eo_out2", "eo_out3", "added", "stored")}
        xn_stored = [sem(f"xn_stored{q}") for q in range(XB)]
        back_in = [sem(f"back_in{k}") for k in range(4)]

        block = ctx.enter_context(nc.Block())

        @block.sync
        def _(sp):
            sp.dma_start(w_down_sb, w_down).then_inc(w_in, 16)
            sp.dma_start(w_up_sb, w_up).then_inc(w_in, 16)
            sp.dma_start(w_q_sb, w_q).then_inc(w_in, 16)
            sp.dma_start(w_out_sb, w_out.rearrange("(g d) c -> d g c", d=P)).then_inc(w_in, 16)
            for k in range(4):
                n = TILES // 4
                sp.dma_start(X[:, k * n:(k + 1) * n, :],
                             x[k * n * P:(k + 1) * n * P, :].rearrange("(t p) c -> p t c", p=P)).then_inc(x_in[k], 16)
            sp.dma_start(Wr_sb[:, :], Wr).then_inc(S["wr_in"], 16)
            def load_g(n):
                seen(sp, S["t_ready"], 2 * n + 2)
                p = (n + 1) % NP
                sp.dma_start(G_cur[:, :, :, :].rearrange("p a h c -> p (a h c)").bitcast(F32),
                             GU[:, bass.ds(p, 1), 0:512].rearrange("p a n -> p (a n)").bitcast(F32)).then_inc(S["g_loaded"], 16)

            def load_u(n):
                seen(sp, S["out_ready"], 2 * n + 2)
                p = (n + 1) % NP
                sp.dma_start(U_cur[:, :, :, :].rearrange("p a h c -> p (a h c)").bitcast(F32),
                             GU[:, bass.ds(p, 1), 512:1024].rearrange("p a n -> p (a n)").bitcast(F32)).then_inc(S["u_loaded"], 16)

            def load_xn(b):
                seen(sp, S["y_ready"], 2 * NP * b)
                sp.dma_start(xn_cur[:, :, :, :].rearrange("p a t c -> p (a t c)").bitcast(F32),
                             xn_dram[bass.ds(b, 1), :, :].rearrange("b p n -> p (b n)")).then_inc(S["xn_loaded"], 16)

            for b in range(B):
                q = b % XB
                sp.wait_ge(S["xnlo_done"], b + 1)
                sp.dma_start(xn_dram[b:b + 1, :, :].rearrange("b p (a n) -> p (b a) n", a=2),
                             PT[:, :, q * T:(q + 1) * T].bitcast(F32)).then_inc(xn_stored[q], 16)
                if b == 4:
                    sp.wait_ge(S["gulo_done"], 1)
                    load_g(-1)
                    load_u(-1)

            for q in range(XB):
                sp.wait_ge(xn_stored[q], 16 * B // XB)
            load_xn(0)
            sp.wait_ge(S["gulo_done"], NP)
            load_g(0)
            load_g(1)

            def load_step(n):
                load_g(n)
                with sp.If((n % NP) == 1):
                    load_xn(n // NP)
                load_u(n - 2)

            with sp.Fori(0, E) as e:
                sp.dma_start(W_ffn[:, bass.ds(e, 1), 0:HID], Wg[bass.ds(e, 1), :, :].rearrange("e c n -> c e n")).then_inc(S["ffn_up_in"], 16)
                sp.dma_start(W_ffn[:, bass.ds(e, 1), HID:2 * HID], Wu[bass.ds(e, 1), :, :].rearrange("e c n -> c e n")).then_inc(S["ffn_up_in"], 16)
                load_step(e + 2)
            sp.wait_ge(S["rows_written"], 16 * FILLS)
            with sp.Fori(0, E) as e:
                sp.dma_start(W_dn[:, bass.ds(e, 1), :, :].rearrange("p e h c -> p (e h) c"),
                             Wd[bass.ds(e, 1), :, :].rearrange("e (h p) c -> p (e h) c", p=P)).then_inc(S["ffn_down_in"], 16)
                load_step(e + 2 + E)
            with sp.Fori(2 * E + 2, STEPS - 1) as n:
                load_step(n)
            load_u(STEPS - 3)
            load_u(STEPS - 2)

            sp.wait_ge(S["table_done"], 1)
            sp.wait_ge(S["rows_written"], 16 * (K * NT * B + FILLS))

            def load_tile(m, q):
                j = RING * m + q
                row = nc.sync.value_load(table[0:1, 1, bass.ds(j, 1)], min_val=0, max_val=E * REGION - P)
                src = rows_dram[bass.ds(nc.sync.snap(row), P), :]
                seen(sp, S["meta_done"], 2 * (j - RING + 1))
                sp.dma_start(x_in_tile[q], src).then_inc(S[f"x_tile_in{q}"], 16)

            for q in range(RING):
                load_tile(0, q)
            with sp.Fori(1, TURNS) as m:
                for q in range(RING):
                    load_tile(m, q)
            for q in range(LEFT):
                load_tile(TURNS, q)
            for q in range(RING):
                sp.wait_ge(S[f"eo_out{q}"], 16 * (TURNS + (q < LEFT)))
            n = TILES // 4
            for k in range(4):
                for a in range(K):
                    r = a * NTOK + k * n * P
                    sp.dma_start(back[:, a, k * n:(k + 1) * n, :],
                                 expert_dram[r:r + n * P, :].rearrange("(t p) c -> p t c", p=P)).then_inc(back_in[k], 16)
            for k in range(4):
                sp.wait_ge(S["added"], 2 * k + 2)
                sp.dma_start(out[k * n * P:(k + 1) * n * P, :].rearrange("(t p) c -> p t c", p=P),
                             X[:, k * n:(k + 1) * n, :]).then_inc(S["stored"], 16)
            sp.wait_ge(S["stored"], 64)

        @block.gpsimd
        def _(pool):
            nc.gpsimd.memset(ident[:, :], 0.0).then_inc(consts, 1)
            nc.gpsimd.memset(mask[:, :], 0.0).then_inc(consts, 1)
            nc.gpsimd.memset(zero_bf[:, :], 0.0).then_inc(consts, 1)
            nc.gpsimd.memset(power[:, :], -0.5).then_inc(consts, 1)
            nc.gpsimd.memset(eps[:, :], EPS)
            nc.gpsimd.memset(W_dn[:, :, :, :].rearrange("p e h c -> p (e h c)")[:, 0:8 * ROW], 0.0).then_inc(S["zero_tile"], 1)
            pool.wait_ge(consts, 2)
            nc.gpsimd.affine_select(out=ident[:, :], in_=ident[:, :], compare_op=ALU.not_equal, fill=1.0,
                                    base=0, pattern=[[-1, P]], channel_multiplier=1).then_inc(consts, 1)
            nc.gpsimd.affine_select(out=mask[:, T - P:T], in_=mask[:, T - P:T], compare_op=ALU.is_ge, fill=MASKED,
                                    base=0, pattern=[[-1, P]], channel_multiplier=1).then_inc(consts, 1)
            nc.gpsimd.memset(before_bf[:, :], 0.0).then_inc(consts, 1)
            nc.gpsimd.memset(ones_bf[:, :], 1.0).then_inc(consts, 1)
            pool.wait_ge(consts, 8)
            nc.gpsimd.affine_select(out=before_bf[:, :], in_=before_bf[:, :], compare_op=ALU.is_ge, fill=1.0,
                                    base=0, pattern=[[-1, P]], channel_multiplier=1).then_inc(consts, 1)
            nc.gpsimd.iota(const_i[:, 0:NT * E], pattern=[[0, NT], [1, E]], base=0, channel_multiplier=0).then_inc(consts, 1)
            pool.wait_ge(consts, 10)
            nc.gpsimd.tensor_copy(expert_id[:, :, :].rearrange("p t e -> p (t e)"), const_i[:, 0:NT * E]).then_inc(consts, 1)
            pool.wait_ge(consts, 11)
            nc.gpsimd.iota(const_i[:, 0:SLOTS], pattern=[[1, SLOTS]], base=0, channel_multiplier=0).then_inc(consts, 1)
            pool.wait_ge(consts, 12)
            nc.gpsimd.tensor_copy(slot_id[:, :], const_i[:, 0:SLOTS]).then_inc(consts, 1)
            pool.wait_ge(consts, 13)
            nc.gpsimd.iota(const_i[:, 0:K * NT], pattern=[[NTOK, K], [P, NT]], base=1 - T, channel_multiplier=1).then_inc(consts, 1)
            pool.wait_ge(consts, 14)
            nc.gpsimd.tensor_copy(dest[:, :, :].rearrange("p k t -> p (k t)"), const_i[:, 0:K * NT]).then_inc(consts, 1)
            pool.wait_ge(consts, 6)

            def xn_rstd(q):
                o = slice(q * TILES // 4, (q + 1) * TILES // 4)
                pool.wait_ge(S["aggr_done"], (q + 1) * TILES // 4)
                nc.gpsimd.tensor_scalar(rstd[:, o], mv[:, o, 1], EPS, None, ALU.add).then_inc(S["rstd_done"], 1)
                pool.wait_ge(S["rstd_done"], 2 * q + 1)
                nc.gpsimd.tensor_tensor(rstd[:, o], rstd[:, o], power[:, o], ALU.pow).then_inc(S["rstd_done"], 1)

            def xn_lo(b):
                q = b % XB
                pool.wait_ge(S["xnhi_done"], b + 1)
                nc.gpsimd.tensor_tensor(PT[:, 1, q * T:(q + 1) * T], xn_f32[:, b % 2, :, :].rearrange("p t c -> p (t c)"),
                                        PT[:, 0, q * T:(q + 1) * T].bitcast(F32), ALU.subtract).then_inc(S["xnlo_done"], 1)

            for do, k in ((xn_rstd, 0), (xn_rstd, 1), (xn_lo, 0), (xn_lo, 1), (xn_rstd, 2), (xn_lo, 2), (xn_lo, 3),
                          (xn_rstd, 3), (xn_lo, 4), (xn_lo, 5), (xn_lo, 6), (xn_lo, 7)):
                do(k)

            def norm(n, i):
                seen(pool, S["inv_done"], 2 * (NT * n + i + 1))
                nc.gpsimd.tensor_tensor(p_pair(i), p_pair(i),
                                        row_inv[:, i, :].unsqueeze(2).to_broadcast([P, 2, P * (i + 1)]),
                                        ALU.mult).then_inc(S["norm_done"], 1)

            def post_rstd(b):
                seen(pool, S["stats2"], 8 * b + 8)
                nc.gpsimd.tensor_tensor(rstd[:, 0:NT], mv[:, 0:NT, 1], eps[:, :], ALU.add).then_inc(S["rstd2"], 1)
                seen(pool, S["rstd2"], 2 * b + 1)
                nc.gpsimd.tensor_tensor(rstd[:, 0:NT], rstd[:, 0:NT], power[:, 0:NT], ALU.pow).then_inc(S["rstd2"], 1)

            def post_scatter(b, first, end):
                if first == 0:
                    seen(pool, S["rows_done"], b + 1)
                    nc.gpsimd.tensor_tensor(gate_p[:, RING:RING + 1], eps[:, 0:1], eps[:, 0:1], ALU.add)
                for k, t in [(k, t) for k in range(K) for t in range(NT)][first:end]:
                    nc.gpsimd.indirect_dma_start(
                        out=rows_dram, out_offset=bass.IndirectOffsetOnAxis(ap=row_i[:, k, t:t + 1], axis=0),
                        in_=routed[:, k, t, :], in_offset=None).then_inc(S["rows_written"], 16)

            def fill(k):
                n = E * REGION // P // 8 // FILLS
                nc.gpsimd.dma_start(
                    rows_dram.rearrange("(k p a r) c -> k p a (r c)", k=FILLS, p=P, a=n)[bass.ds(k, 1), :, :, :].rearrange("k p a n -> p (k a) n"),
                    W_dn[:, :, :, :].rearrange("p e h c -> p (e h c)")[:, 0:8 * ROW].unsqueeze(1).to_broadcast([P, n, 8 * ROW])
                    ).then_inc(S["rows_written"], 16)

            pool.wait_ge(S["zero_tile"], 1)
            for i in range(NT - 1):
                norm(0, i)
            with pool.Fori(1, NP + 1) as n:
                norm(n - 1, 3)
                fill(n - 1)
                for i in range(NT - 1):
                    norm(n, i)

            def step(n, k, b):
                if k == 3:
                    post_rstd(b)
                if k in (7, 8):
                    post_scatter(b, 4 * (k - 7), 4 * (k - 7) + 2)
                norm(n - 1, 3)
                if k in (7, 8):
                    post_scatter(b, 4 * (k - 7) + 2, 4 * (k - 7) + 4)
                for i in range(NT - 1):
                    norm(n, i)

            pool.wait_ge(S["rows_written"], 16 * FILLS)
            with pool.Fori(1, B - 1) as m:
                for k in range(1, NP + 1):
                    step(NP * m + k, k, m - 1)
            for k in range(1, NP - 1):
                step(NP * (B - 1) + k, k, B - 2)
            norm(STEPS - 2, 3)
            for i in range(NT):
                norm(STEPS - 1, i)
            post_scatter(B - 2, 0, 8)
            post_rstd(B - 1)
            post_scatter(B - 1, 0, 8)

            def scatter_tile(m, q):
                j = RING * m + q
                seen(pool, S["eo_done"], j + 1)
                nc.gpsimd.tensor_tensor(gate_p[:, q:q + 1], eps[:, 0:1], eps[:, 0:1], ALU.add)\
                    .then_inc(S["gated"], 1)
                nc.gpsimd.indirect_dma_start(
                    out=expert_dram, out_offset=bass.IndirectOffsetOnAxis(ap=meta_row[:, q:q + 1], axis=0),
                    in_=eo_sb[q % 2], in_offset=None, bounds_check=K * NTOK - 1, oob_is_err=False).then_inc(S[f"eo_out{q}"], 16)

            for q in range(RING):
                scatter_tile(0, q)
            with pool.Fori(1, TURNS) as m:
                for q in range(RING):
                    scatter_tile(m, q)
            for q in range(LEFT):
                scatter_tile(TURNS, q)

        @block.scalar
        def _(act):
            act.wait_ge(S["wdT_ready"], 1)
            nc.scalar.activation(wdT[:, :], post_ps[:, 0:P], ACT.Copy).then_inc(S["wdT_copied"], 1)

            def wT_copy(g):
                act.wait_ge(S["wT_ready"], g + 1)
                if g > 1:
                    act.wait_ge(S["gu_ready"], g - 1)
                nc.scalar.activation(wT[g % 2], s_ps[0][:, 0:3 * P], ACT.Copy).then_inc(S["wT_copied"], 1)

            def gu_hi(g):
                act.wait_ge(S["gu_ready"], g + 1)
                for h in range(2):
                    last = nc.scalar.activation(gu_at(g, 0, h), gu_ps[g % 2][h], ACT.Copy)
                last.then_inc(S["guhi_done"], 1)

            def xn_hi(b):
                q = b % XB
                act.wait_ge(S["xn_done"], 4 * b + 4)
                if b >= XB:
                    act.wait_ge(xn_stored[q], 16 * (b // XB))
                nc.scalar.activation(PT[:, 0, q * T:(q + 1) * T], xn_f32[:, b % 2, :, :].rearrange("p t c -> p (t c)"),
                                     ACT.Copy).then_inc(S["xnhi_done"], 1)
                act.wait_ge(S["xT_ready"], b + 1)
                nc.scalar.activation(XT[:, 0, b * T:(b + 1) * T], xT_ps[b % 2], ACT.Copy).then_inc(S["xThi_done"], 1)

            wT_copy(0)
            for g in range(NP):
                if g < NP - 1:
                    wT_copy(g + 1)
                gu_hi(g)
                if g >= 2:
                    xn_hi(g - 2)
            xn_hi(B - 2)
            xn_hi(B - 1)

            def t_hi(n, h):
                seen(act, S["t_ready"], 2 * n + h + 1)
                seen(act, S["s_ready"], 8 * n)
                nc.scalar.activation(t_sb[:, 0, h, :], t_ps[h][:, :], ACT.Copy).then_inc(S["thi_done"], 1)

            def exps(n, i, h):
                seen(act, S["max_done"], 8 * n + 2 * i + h + 1)
                seen(act, S["inv_done"], 2 * (NT * (n - 1) + i) + h + 1)
                nc.scalar.activation(p_at(i, h), p_at(i, h), ACT.Exp, bias=neg_max[:, i, h:h + 1], scale=-1.0,
                                     accum_out=row_sum[:, i, h:h + 1]).then_inc(S["exp_done"], 1)

            def pt_hi(n, u):
                seen(act, S["pt_ready"], NPT * n + u + 1)
                seen(act, S["y_ready"], 2 * (n - 1) + PARTS[u][0] // 2 + 1)
                nc.scalar.activation(pt_part(u, 0), pt_part(u), ACT.Copy).then_inc(S["pthi_done"], 1)

            def y_hi(n, half):
                seen(act, S["y_ready"], 2 * n + half + 1)
                seen(act, S["out_ready"], 2 * n)
                nc.scalar.activation(y_sb[:, 0, :, half * 256:(half + 1) * 256], y_ps[half][:, :].rearrange("p (h q) -> p h q", h=2), ACT.Copy)\
                    .then_inc(S["yhi_done"], 1)

            def step(n, cur=True, prev=True, prev2=True, nxt=True, k=None, b=None):
                if prev:
                    pt_hi(n - 1, 0)
                if prev2:
                    y_hi(n - 2, 1)
                if prev:
                    pt_hi(n - 1, 1)
                if cur:
                    exps(n, 0, 0)
                    exps(n, 0, 1)
                if k == 6:
                    post_gap(b)
                if prev:
                    pt_hi(n - 1, 2)
                    pt_hi(n - 1, 3)
                if cur:
                    exps(n, 1, 0)
                    exps(n, 1, 1)
                if prev:
                    pt_hi(n - 1, 4)
                    pt_hi(n - 1, 5)
                if cur:
                    exps(n, 2, 0)
                    exps(n, 2, 1)
                if nxt:
                    t_hi(n + 1, 0)
                if cur:
                    exps(n, 3, 0)
                if nxt:
                    t_hi(n + 1, 1)
                if prev:
                    y_hi(n - 1, 0)
                if cur:
                    exps(n, 3, 1)
                if k == 1:
                    post_out(b)
                if k == 4:
                    post_xn2T(b)

            def split_weights(k):
                if k == 2:
                    act.wait_ge(S["ffn_up_in"], 32 * E)
                for e in SPLIT_HI[HI_AT.get(k - 1, 0):HI_AT[k]]:
                    act.wait_ge(S["g_loaded"], 16 * (STEPS - NP + e + 1))
                    act.wait_ge(S["u_loaded"], 16 * (STEPS - NP + e + 1))
                    nc.scalar.activation(up_hi[:, e, :], W_ffn[:, e, :], ACT.Copy).then_inc(S["split_hi"], 1)

            def post_out(b):
                act.wait_ge(S["out_ready"], 16 * (b + 1))
                nc.scalar.activation(outT[:, :], out_ps[:, :], ACT.Copy).then_inc(S["outT_copied"], 1)

            def post_xn2T(b):
                seen(act, S["xn2T_ready"], b + 1)
                nc.scalar.activation(xn2T[:, :], post_ps[:, :], ACT.Copy).then_inc(S["xn2T_copied"], 1)
                seen(act, S["xn2_done"], 4 * b + 4)
                nc.scalar.activation(routed[:, 1, :, 0:C], routed[:, 0, :, 0:C], ACT.Copy).then_inc(S["rows_copied"], 1)

            def post_gap(b):
                seen(act, S["gap_done"], b + 1)
                nc.scalar.activation(gap_exp[:, :], gap[:, :], ACT.Exp).then_inc(S["gap_exp_done"], 1)

            t_hi(0, 0)
            t_hi(0, 1)
            for q in range(XB):
                act.wait_ge(xn_stored[q], 16 * B // XB)
            step(0, prev=False, prev2=False)
            step(1, prev2=False)
            with act.Fori(2, NP + 1) as n:
                step(n)
            with act.Fori(1, B - 1) as m:
                for k in range(1, NP + 1):
                    step(NP * m + k, k=k, b=m - 1)
            for k in range(1, NP - 1):
                step(NP * (B - 1) + k, k=k, b=B - 2)
                if k > 1:
                    split_weights(k)
            step(STEPS - 1, nxt=False)
            split_weights(NP - 1)
            step(STEPS, cur=False, nxt=False)
            split_weights(NP)
            step(STEPS + 1, cur=False, prev=False, nxt=False)
            post_out(B - 1)
            split_weights(NP + 1)
            post_xn2T(B - 1)
            post_gap(B - 1)

            def tile_xT(m, q):
                j = RING * m + q
                seen(act, S["x_tile_T"], j + 1)
                seen(act, S["u_ready"], j - 1)
                nc.scalar.activation(xT_tile[q % 2][:, 0, :], post_ps[:, 0:P], ACT.Copy).then_inc(S["x_hi"], 1)

            def tile_silu(m, q):
                j = RING * m + q
                seen(act, S["g_ready"], j + 1)
                seen(act, S["h_done"], j - 1)
                nc.scalar.activation(silu_sb[q % 2], g_ps[q % 2], ACT.Silu).then_inc(S["silu_done"], 1)

            def tile_hT(m, q):
                j = RING * m + q
                seen(act, S["hT_ready"], j + 1)
                seen(act, S["eo_ready"], j - 1)
                nc.scalar.activation(hT_sb[q % 2][:, :], out_ps[:, :], ACT.Copy).then_inc(S["hT_copied"], 1)

            def turn(m, q, first=False, last=False, drain=False):
                if not last and not drain:
                    tile_xT(*after(m, q))
                if not first:
                    tile_hT(*before(m, q))
                if not drain:
                    tile_silu(m, q)

            tile_xT(0, 0)
            for q in range(RING):
                turn(0, q, first=(q == 0))
            with act.Fori(1, TURNS) as m:
                for q in range(RING):
                    turn(m, q)
            for q in range(LEFT):
                turn(TURNS, q, last=(q == LEFT - 1))
            turn(TURNS, LEFT, drain=True)

        @block.vector
        def _(dve):
            dve.wait_ge(consts, 6)

            def xn_stats(q):
                n = TILES // 4
                dve.wait_ge(x_in[q], 16)
                for t in range(q * n, (q + 1) * n):
                    nc.vector.bn_stats(stats[:, t, :], X[:, t, :]).then_inc(S["stats_done"], 1)
                for t in range(q * n, (q + 1) * n):
                    dve.wait_ge(S["stats_done"], t + 1)
                    nc.vector.bn_aggr(mv[:, t, :], stats[:, t, :]).then_inc(S["aggr_done"], 1)

            def gu_lo(g):
                dve.wait_ge(S["guhi_done"], g + 1)
                for h in range(2):
                    last = nc.vector.tensor_tensor(gu_at(g, 1, h), gu_ps[g % 2][h], gu_at(g, 0, h).bitcast(F32), ALU.subtract)
                last.then_inc(S["gulo_done"], 1)

            def normalise(b):
                dve.wait_ge(S["rstd_done"], 2 * (b // 2 + 1))
                if b > 1:
                    dve.wait_ge(S["xT_ready"], b - 1)
                    dve.wait_ge(S["xnlo_done"], b - 1)
                for t in range(NT):
                    nc.vector.tensor_scalar(xn_f32[:, b % 2, t, :], X[:, NT * b + t, :], mv[:, NT * b + t, 0:1],
                                            rstd[:, NT * b + t:NT * b + t + 1], ALU.subtract, ALU.mult).then_inc(S["xn_done"], 1)

            def xT_lo(b):
                dve.wait_ge(S["xThi_done"], b + 1)
                o = slice(b * T, (b + 1) * T)
                nc.vector.tensor_tensor(XT[:, 1, o], xT_ps[b % 2], XT[:, 0, o].bitcast(F32), ALU.subtract).then_inc(S["xTlo_done"], 1)

            xn_stats(0)
            gu_lo(0)
            xn_stats(1)
            gu_lo(1)
            normalise(0)
            for g in range(2, NP):
                gu_lo(g)
                if g in (3, 5):
                    xn_stats((g + 1) // 2)
                normalise(g - 1)
                xT_lo(g - 2)
            normalise(B - 1)
            xT_lo(B - 2)
            xT_lo(B - 1)

            def t_lo(n, h):
                seen(dve, S["thi_done"], 2 * n + h + 1)
                nc.vector.tensor_tensor(t_sb[:, 1, h, :], t_ps[h][:, :], t_sb[:, 0, h, :].bitcast(F32), ALU.subtract)\
                    .then_inc(S["tlo_done"], 1)

            def maxes(n, i):
                seen(dve, S["pt_ready"], NPT * (n - 1) + parts_to[i])
                w = P * (i + 1)
                for h in range(2):
                    seen(dve, S["s_ready"], 8 * n + 2 * i + h + 1)
                    if i:
                        inv(n, i - 1, h)
                    else:
                        inv(n - 1, NT - 1, h)
                    nc.vector.tensor_tensor_reduce(out=p_at(i, h), in0=s_ps[h][:, 0:w], in1=mask[:, T - w:T],
                                                   scale=-SCALE, scalar=BIG, op0=ALU.add, op1=ALU.min,
                                                   accum_out=neg_max[:, i, h:h + 1]).then_inc(S["max_done"], 1)

            def inv(n, i, h):
                if isinstance(n, int) and n < 0:
                    return
                seen(dve, S["norm_done"], NT * (n - 1) + i + 1)
                seen(dve, S["exp_done"], 8 * n + 2 * i + h + 1)
                nc.vector.reciprocal(row_inv[:, i, h:h + 1], row_sum[:, i, h:h + 1]).then_inc(S["inv_done"], 1)

            def pt_lo(n, u):
                seen(dve, S["pthi_done"], NPT * n + u + 1)
                nc.vector.tensor_tensor(pt_part(u, 1), pt_part(u), pt_part(u, 0).bitcast(F32), ALU.subtract)\
                    .then_inc(S["ptlo_done"], 1)

            def y_lo(n, half):
                seen(dve, S["yhi_done"], 2 * n + half + 1)
                o = slice(half * 256, (half + 1) * 256)
                nc.vector.tensor_tensor(y_sb[:, 1, :, o], y_ps[half][:, :].rearrange("p (h q) -> p h q", h=2), y_sb[:, 0, :, o].bitcast(F32), ALU.subtract)\
                    .then_inc(S["ylo_done"], 1)

            def step(n, cur=True, prev=True, prev2=True, nxt=True, k=None, b=None):
                if prev:
                    pt_lo(n - 1, 0)
                if cur:
                    maxes(n, 0)
                elif prev:
                    inv(n - 1, NT - 1, 0)
                    inv(n - 1, NT - 1, 1)
                if prev2:
                    y_lo(n - 2, 1)
                if prev:
                    pt_lo(n - 1, 1)
                if cur:
                    maxes(n, 1)
                if prev:
                    pt_lo(n - 1, 2)
                    pt_lo(n - 1, 3)
                if cur:
                    maxes(n, 2)
                if prev:
                    pt_lo(n - 1, 4)
                    pt_lo(n - 1, 5)
                if cur:
                    maxes(n, 3)
                if nxt:
                    t_lo(n + 1, 0)
                    t_lo(n + 1, 1)
                if prev:
                    y_lo(n - 1, 0)
                if k == 2:
                    post_x2(b)
                if k == 3:
                    post_xn2(b)
                if k == 5:
                    post_choose(b)
                if k == 6:
                    post_rows(b)

            def split_weights(k):
                if k == NP + 1:
                    dve.wait_ge(S["s_ready"], 8 * STEPS)
                for e in SPLIT_LO[LO_AT.get(k - 1, 0):LO_AT[k]]:
                    dve.wait_ge(S["split_hi"], SPLIT_HI.index(e) + 1)
                    nc.vector.tensor_tensor(up_lo[:, e, :], W_ffn[:, e, :], up_hi[:, e, :].bitcast(F32), ALU.subtract)\
                        .then_inc(S["split_lo"], 1)

            def post_x2(b):
                seen(dve, S["outT_ready"], b + 1)
                xs = X[:, bass.ds(4 * b, 4), :].rearrange("p a c -> p (a c)")
                nc.vector.tensor_tensor(xs, post_ps[:, :], xs, ALU.add).then_inc(S["x2_done"], 1)
                seen(dve, S["x2_done"], b + 1)
                nc.vector.tensor_scalar(dest[:, :, :], dest[:, :, :], float(T), None, ALU.add).then_inc(S["dest_done"], 1)
                for t in range(NT):
                    nc.vector.bn_stats(stats[:, t, :], X[:, bass.ds(4 * b + t, 1), :].rearrange("p a c -> p (a c)"))\
                        .then_inc(S["stats2"], 1)
                seen(dve, S["stats2"], 8 * b + 4)
                nc.vector.memset(gate_v[:, :], 0)
                for t in range(NT):
                    nc.vector.bn_aggr(mv[:, t, :], stats[:, t, :]).then_inc(S["stats2"], 1)

            def post_xn2(b):
                seen(dve, S["rstd2"], 2 * b + 2)
                seen(dve, S["rows_written"], 16 * (K * NT * b + FILLS))
                for t in range(NT):
                    nc.vector.tensor_scalar(routed[:, 0, t, 0:C], X[:, bass.ds(4 * b + t, 1), :].rearrange("p a c -> p (a c)"),
                                            mv[:, t, 0:1], rstd[:, t:t + 1], ALU.subtract, ALU.mult).then_inc(S["xn2_done"], 1)

            ROUTING = 21

            def post_choose(b):
                def made(k):
                    seen(dve, S["routing"], ROUTING * b + k)

                def sig(ins):
                    ins.then_inc(S["routing"], 1)

                seen(dve, S["logits_ready"], b + 1)
                sig(nc.vector.tensor_copy(logit[:, :, :].rearrange("p t e -> p (t e)"), post_ps[:, 0:NT * E]))
                for t in range(NT):
                    sig(nc.vector.max(top[:, t, :], post_ps[:, t * E:(t + 1) * E]))
                made(5)
                nc.vector.tensor_tensor(gap[:, :], top[:, :, 1], top[:, :, 0], ALU.subtract).then_inc(S["gap_done"], 1)
                for t in range(NT):
                    sig(nc.vector.max_index(top_i[:, t, :], top[:, t, :], logit[:, t, :]))
                made(9)
                sig(nc.vector.tensor_copy(top_f[:, :, :], top_i[:, :, 0:K]))
                made(10)
                for k in range(K):
                    sig(nc.vector.tensor_tensor(chosen[:, k, :, :], expert_id[:, :, :],
                                                top_f[:, :, k].unsqueeze(2).to_broadcast([P, NT, E]), ALU.is_equal))
                made(12)
                nc.vector.tensor_tensor(chosen_bf[:, :, :], chosen[:, 0, :, :], chosen[:, 1, :, :], ALU.add)\
                    .then_inc(S["chosen_done"], 1)

            def post_rows(b):
                def made(k):
                    seen(dve, S["routing"], ROUTING * b + k)

                def sig(ins):
                    ins.then_inc(S["routing"], 1)

                seen(dve, S["ranks_ready"], b + 1)
                sig(nc.vector.tensor_tensor(pos[:, :, :], post_ps[:, RANK_COL:RANK_COL + NT * E].rearrange("p (t e) -> p t e", e=E),
                                            base[:, :].unsqueeze(1).to_broadcast([P, NT, E]), ALU.add))
                made(13)
                sig(nc.vector.tensor_tensor(base[:, :], post_ps[:, TOTAL_COL:TOTAL_COL + E], base[:, :], ALU.add))
                for k in range(K):
                    sig(nc.vector.tensor_tensor(picked[:, k, :, :], chosen[:, k, :, :], pos[:, :, :], ALU.mult))
                made(16)
                sig(nc.vector.tensor_reduce(row_f[:, :, :], picked[:, :, :, :], AX.X, ALU.add))
                seen(dve, S["gap_exp_done"], b + 1)
                sig(nc.vector.tensor_scalar(weight[:, 1, :], gap_exp[:, :], 1.0, None, ALU.add))
                made(18)
                sig(nc.vector.reciprocal(weight[:, 0, :], weight[:, 1, :]))
                sig(nc.vector.tensor_copy(row_i[:, :, :], row_f[:, :, :]))
                made(19)
                sig(nc.vector.tensor_tensor(weight[:, 1, :], gap_exp[:, :], weight[:, 0, :], ALU.mult))
                made(21)
                nc.vector.tensor_scalar(routed[:, :, :, C], weight[:, :, :], DEPTH_SCALE, None, ALU.mult)
                seen(dve, S["rows_copied"], b + 1)
                seen(dve, S["dest_done"], b + 1)
                nc.vector.tensor_copy(routed[:, :, :, C + 1], dest[:, :, :]).then_inc(S["rows_done"], 1)

            nc.vector.tensor_scalar(base[:, :], expert_id[:, 0, :], float(REGION), None, ALU.mult).then_inc(S["base_set"], 1)
            dve.wait_ge(S["base_set"], 1)
            dve.wait_ge(S["xnlo_done"], B)
            t_lo(0, 0)
            t_lo(0, 1)
            step(0, prev=False, prev2=False)
            step(1, prev2=False)
            with dve.Fori(2, NP + 1) as n:
                step(n)
            with dve.Fori(1, B - 1) as m:
                for k in range(1, NP + 1):
                    step(NP * m + k, k=k, b=m - 1)
            for k in range(1, NP - 1):
                step(NP * (B - 1) + k, k=k, b=B - 2)
                if k > 1:
                    split_weights(k)
            step(STEPS - 1, nxt=False)
            split_weights(NP - 1)
            step(STEPS, cur=False, nxt=False)
            split_weights(NP)
            step(STEPS + 1, cur=False, prev=False, nxt=False)
            post_x2(B - 1)
            split_weights(NP + 1)
            post_xn2(B - 1)
            post_choose(B - 1)
            post_rows(B - 1)

            tabled = [0]

            def tab(ins):
                tabled[0] += 1
                ins.then_inc(S["tabling"], 1)
                dve.wait_ge(S["tabling"], tabled[0])

            tab(nc.vector.scalar_tensor_tensor(count[:, :], expert_id[0:1, 0, :], float(-REGION), base[0:1, :], ALU.mult, ALU.add))
            tab(nc.vector.tensor_scalar(count_i[:, :], count[:, :], float(P - 1), None, ALU.add))
            tab(nc.vector.tensor_single_scalar(count_i[:, :], count_i[:, :], 7, op=ALU.arith_shift_right))
            tab(nc.vector.tensor_copy(tiles_of[:, :], count_i[:, :]))
            tab(nc.vector.tensor_copy(ends[:, :], tiles_of[:, :]))
            for e in range(1, E):
                tab(nc.vector.tensor_tensor(ends[:, e:e + 1], ends[:, e - 1:e], ends[:, e:e + 1], ALU.add))
            tab(nc.vector.tensor_scalar(jump[:, :], tiles_of[:, :], float(-P), float(REGION), ALU.mult, ALU.add))
            shape = [1, SLOTS, E - 1]
            tab(nc.vector.tensor_tensor(past[:, :, :], slot_id[0:1, :].unsqueeze(2).to_broadcast(shape),
                                        ends[:, 0:E - 1].unsqueeze(1).to_broadcast(shape), ALU.is_ge))
            tab(nc.vector.tensor_tensor(jumps[:, :, :], past[:, :, :], jump[:, 0:E - 1].unsqueeze(1).to_broadcast(shape), ALU.mult))
            tab(nc.vector.tensor_reduce(table_f[:, 0, :], past[:, :, :], AX.X, ALU.add))
            tab(nc.vector.tensor_reduce(table_f[:, 1, :], jumps[:, :, :], AX.X, ALU.add))
            tab(nc.vector.scalar_tensor_tensor(table_f[:, 1, :], slot_id[0:1, :], float(P), table_f[:, 1, :], ALU.mult, ALU.add))
            tab(nc.vector.tensor_scalar(table_f[:, 1, :], table_f[:, 1, :], float(E * REGION - P), None, ALU.min))
            nc.vector.tensor_copy(table[:, :, :], table_f[:, :, :]).then_inc(S["table_done"], 1)

            def tile_xT(m, q):
                j = RING * m + q
                seen(dve, S["x_hi"], j + 1)
                nc.vector.tensor_tensor(xT_tile[q % 2][:, 1, :], post_ps[:, 0:P], xT_tile[q % 2][:, 0, :].bitcast(F32), ALU.subtract)\
                    .then_inc(S["x_lo"], 1)

            def tile_meta(m, q):
                j = RING * m + q
                seen(dve, S[f"x_tile_in{q}"], 16 * (m + 1))
                seen(dve, S["gated"], j - RING + 1)
                seen(dve, S[f"eo_out{q}"], 16 * m)
                nc.vector.tensor_copy(meta_w[:, q:q + 1], x_in_tile[q][:, C:C + 1]).then_inc(S["meta_done"], 1)
                nc.vector.tensor_scalar(meta_row[:, q:q + 1], x_in_tile[q][:, C + 1:C + 2], -1.0, None, ALU.add)\
                    .then_inc(S["meta_done"], 1)

            def tile_h(m, q):
                j = RING * m + q
                seen(dve, S["silu_done"], j + 1)
                seen(dve, S["u_ready"], j + 1)
                seen(dve, S["hT_ready"], j - 1)
                nc.vector.tensor_tensor(h_sb[q % 2], u_ps[q % 2], silu_sb[q % 2], ALU.mult).then_inc(S["h_done"], 1)

            def tile_eo(m, q):
                j = RING * m + q
                seen(dve, S["eo_ready"], j + 1)
                seen(dve, S["meta_done"], 2 * (j + 1))
                seen(dve, S[f"eo_out{(q - 2) % RING}"], 16 * (m + 1) if q >= 2 else 16 * m)
                nc.vector.tensor_scalar(eo_sb[q % 2], eo_ps[q % 2], meta_w[:, q:q + 1], None, ALU.mult).then_inc(S["eo_done"], 1)

            def turn(m, q, first=False, last=False, drain=False):
                if not last and not drain:
                    tile_xT(*after(m, q))
                    tile_meta(*after(m, q))
                if not drain:
                    tile_h(m, q)
                if not first:
                    tile_eo(*before(m, q))

            tile_xT(0, 0)
            tile_meta(0, 0)
            for q in range(RING):
                turn(0, q, first=(q == 0))
            with dve.Fori(1, TURNS) as m:
                for q in range(RING):
                    turn(m, q)
            for q in range(LEFT):
                turn(TURNS, q, last=(q == LEFT - 1))
            turn(TURNS, LEFT, drain=True)

            n = TILES // 4
            for k in range(4):
                xs = X[:, k * n:(k + 1) * n, :]
                dve.wait_ge(back_in[k], 32)
                nc.vector.tensor_tensor(xs, back[:, 0, k * n:(k + 1) * n, :], xs, ALU.add).then_inc(S["added"], 1)
                dve.wait_ge(S["added"], 2 * k + 1)
                nc.vector.tensor_tensor(xs, back[:, 1, k * n:(k + 1) * n, :], xs, ALU.add).then_inc(S["added"], 1)

        @block.tensor
        def _(pe):
            pe.wait_ge(consts, 6)
            pe.wait_ge(w_in, 64)
            nc.tensor.transpose(post_ps[:, 0:P], w_down_sb, ident[:, :]).then_inc(S["wdT_ready"], 1)
            pe.wait_ge(S["wdT_copied"], 1)

            def weights_T(g):
                if g:
                    pe.wait_ge(S["wT_copied"], g)
                nc.tensor.transpose(s_ps[0][:, 0:P], w_q_sb[:, g * P:(g + 1) * P], ident[:, :])
                nc.tensor.matmul(s_ps[0][:, P:2 * P], w_up_sb[:, g * P:(g + 1) * P], wdT[:, :], start=True, stop=True)
                nc.tensor.matmul(s_ps[0][:, 2 * P:3 * P], w_up_sb[:, NH * HD + g * P:NH * HD + (g + 1) * P], wdT[:, :],
                                 start=True, stop=True).then_inc(S["wT_ready"], 1)

            def make_gu(g):
                pe.wait_ge(S["wT_copied"], g + 1)
                if g > 1:
                    pe.wait_ge(S["gulo_done"], g - 1)
                for h in range(2):
                    k = slice(h * HD, (h + 1) * HD)
                    wq, wk, wv = (wT[g % 2][k, i * P:(i + 1) * P] for i in range(3))
                    nc.tensor.matmul(gu_ps[g % 2][h][:, 0, :], wq, wk, start=True, stop=True)
                    last = nc.tensor.matmul(gu_ps[g % 2][h][:, 1, :], wv, w_out_sb[k, g, :], start=True, stop=True)
                last.then_inc(S["gu_ready"], 1)

            def transpose_xn(b):
                pe.wait_ge(S["xn_done"], 4 * b + 4)
                if b > 1:
                    pe.wait_ge(S["xTlo_done"], b - 1)
                for t in range(NT):
                    last = nc.tensor.transpose(xT_ps[b % 2][:, t * P:(t + 1) * P], xn_f32[:, b % 2, t, :], ident[:, :])
                last.then_inc(S["xT_ready"], 1)

            weights_T(0)
            for g in range(NP):
                if g < NP - 1:
                    weights_T(g + 1)
                make_gu(g)
                if g >= 2:
                    transpose_xn(g - 2)
            transpose_xn(B - 2)
            transpose_xn(B - 1)

            def passes(dst, ws, vs, start, stop, **kw):
                nc.tensor.matmul(dst, ws[0], vs[0], start=start, stop=False, **kw)
                nc.tensor.matmul(dst, ws[1], vs[0], start=False, stop=False, **kw)
                return nc.tensor.matmul(dst, ws[0], vs[1], start=False, stop=stop, **kw)

            def xT_at(part, b, w):
                return XT[:, part, bass.ds(b * T, w)]

            def project(n, h, b):
                seen(pe, S["g_loaded"], 16 * (n + 1))
                seen(pe, S["ptlo_done"], NPT * (n - 2) + (4 if h == 0 else 3))
                passes(t_ps[h][:, :], [G_cur[:, a, h, :] for a in range(2)], [xT_at(a, b, T) for a in range(2)],
                       True, True).then_inc(S["t_ready"], 1)

            def scores(n, i, b):
                w = max(256, P * (i + 1))
                for h in range(2):
                    if i == 0:
                        seen(pe, S["tlo_done"], 2 * n + h + 1)
                    seen(pe, S["max_done"], 8 * n + 2 * i + h - 1)
                    passes(s_ps[h][:, 0:w], [t_sb[:, a, h, i * P:(i + 1) * P] for a in range(2)],
                           [xT_at(a, b, w) for a in range(2)], True, True).then_inc(S["s_ready"], 1)

            def transposes(n, i, h=None):
                seen(pe, S["norm_done"], NT * n + i + 1)
                for u in range(parts_to[i - 1] if i else 0, parts_to[i]) if h is None else [parts_to[i - 1] + h]:
                    name, count = [("ptlo_done", NPT * n), ("ylo_done", 2 * n - 1), ("tlo_done", 2 * n + 4),
                                   ("ylo_done", 2 * n), ("ptlo_done", NPT * n + 2), ("ptlo_done", NPT * n + 1)][u]
                    seen(pe, S[name], min(count, 2 * STEPS) if isinstance(n, int) and name == "tlo_done" else count)
                    dst, of = pt_part(u), PARTS[u][1]
                    for g in range(2) if of is None else [of]:
                        for j in range(i + 1):
                            last = nc.tensor.transpose(dst[:, g, j, :] if of is None else dst[:, j, :],
                                                       p_at(i, g)[:, j * P:(j + 1) * P], ident[:, :])
                    last.then_inc(S["pt_ready"], 1)

            def values(n, half, b):
                seen(pe, S["ptlo_done"], NPT * n + (5 if half == 0 else 6))
                if half == 1:
                    seen(pe, S["tlo_done"], min(2 * n + 5, 2 * STEPS) if isinstance(n, int) else 2 * n + 5)
                seen(pe, S["xn_loaded"], 16 * (b + 1))
                keys = 2 * half + 2
                for j in range(keys):
                    if j < keys - 1:
                        dst = y_ps[half][:, :]
                        src = [pt_at(a, half)[:, j, :, :, :].rearrange("p h i q -> p (h i q)") for a in range(2)]
                    else:
                        dst = y_ps[half][:, :].rearrange("p (h q) -> p h q", h=2)[:, :, P:256]
                        src = [pt_at(a, half)[:, j, :, 1, :] for a in range(2)]
                    last = passes(dst, [xn_cur[:, a, j, :] for a in range(2)], src, j == 0, j == keys - 1)
                last.then_inc(S["y_ready"], 1)

            def project_out(n, h):
                if h == 0:
                    seen(pe, S["u_loaded"], 16 * (n + 1))
                    seen(pe, S["ylo_done"], 2 * n + 2)
                passes(out_ps[:, :], [U_cur[:, a, h, :] for a in range(2)], [y_sb[:, a, h, :] for a in range(2)],
                       False, True, skip_group_check=True).then_inc(S["out_ready"], 1)

            def clear_out():
                nc.tensor.matmul(out_ps[:, :], zero_bf[:, 0:P], zero_bf[:, :], start=True, stop=True)

            def step(m, k, cur=True, prev=True, prev2=True, nxt=True, b=None):
                n = NP * m + k
                if prev:
                    transposes(n - 1, 0)
                if prev2:
                    values(n - 2, 1, m + (k - 2) // NP)
                if cur:
                    scores(n, 0, m + k // NP)
                if prev:
                    transposes(n - 1, 1)
                    transposes(n - 1, 2, 0)
                if cur:
                    scores(n, 1, m + k // NP)
                if prev:
                    transposes(n - 1, 2, 1)
                if b is not None:
                    if k == 2:
                        post_out(b)
                    if k == 4:
                        post_xn2T(b)
                    if k == 5:
                        post_logits(b)
                    if k == 6:
                        post_ranks(b)
                if prev2:
                    project_out(n - 2, 0)
                if cur:
                    scores(n, 2, m + k // NP)
                if prev2:
                    project_out(n - 2, 1)
                if prev:
                    transposes(n - 1, 3)
                if cur:
                    scores(n, 3, m + k // NP)
                if nxt:
                    project(n + 1, 0, m + (k + 1) // NP)
                    project(n + 1, 1, m + (k + 1) // NP)
                if prev:
                    values(n - 1, 0, m + (k - 1) // NP)

            def post_out(b, clear=True):
                pe.wait_ge(S["outT_copied"], b + 1)
                if clear:
                    clear_out()
                for t in range(NT):
                    last = nc.tensor.transpose(post_ps[:, t * P:(t + 1) * P], outT[:, t * P:(t + 1) * P], ident[:, :])
                last.then_inc(S["outT_ready"], 1)

            def post_xn2T(b):
                seen(pe, S["xn2_done"], 4 * b + 4)
                seen(pe, S["x2_done"], b + 1)
                for t in range(NT):
                    last = nc.tensor.transpose(post_ps[:, t * P:(t + 1) * P], routed[:, 0, t, 0:C], ident[:, :])
                last.then_inc(S["xn2T_ready"], 1)

            def post_logits(b):
                pe.wait_ge(S["wr_in"], 16)
                seen(pe, S["xn2T_copied"], b + 1)
                for t in range(NT):
                    last = nc.tensor.matmul(post_ps[:, t * E:(t + 1) * E], xn2T[:, t * P:(t + 1) * P], Wr_sb[:, :],
                                            start=True, stop=True)
                last.then_inc(S["logits_ready"], 1)

            def post_ranks(b):
                seen(pe, S["chosen_done"], b + 1)
                ranks = post_ps[:, RANK_COL:RANK_COL + NT * E].rearrange("p (t e) -> p t e", e=E)
                total = post_ps[:, TOTAL_COL:TOTAL_COL + E]
                kw = dict(skip_group_check=True)
                nc.tensor.matmul(ranks, before_bf[:, :], chosen_bf[:, :, :], start=True, stop=True, **kw)
                for t in range(NT - 1):
                    nc.tensor.matmul(ranks[:, t + 1:NT, :], ones_bf[:, :],
                                     chosen_bf[:, t:t + 1, :].to_broadcast([P, NT - 1 - t, E]), start=False, stop=True, **kw)
                for t in range(NT):
                    last = nc.tensor.matmul(total, ones_bf[:, :], chosen_bf[:, t, :], start=False, stop=True, **kw)
                last.then_inc(S["ranks_ready"], 1)

            pe.wait_ge(S["xTlo_done"], B)
            clear_out()
            project(0, 0, 0)
            project(0, 1, 0)
            step(0, 0, prev=False, prev2=False)
            step(0, 1, prev2=False)
            with pe.Fori(2, NP + 1) as k:
                step(0, k)
            with pe.Fori(1, B - 1) as m:
                for k in range(1, NP + 1):
                    step(m, k, b=m - 1)
            for k in range(1, NP - 1):
                step(B - 1, k, b=B - 2)
            step(B - 1, NP - 1, nxt=False)
            step(B - 1, NP, cur=False, nxt=False)
            step(B - 1, NP + 1, cur=False, prev=False, nxt=False)
            post_out(B - 1, clear=False)
            post_xn2T(B - 1)
            post_logits(B - 1)
            post_ranks(B - 1)

            def tile_xT(m, q):
                j = RING * m + q
                seen(pe, S[f"x_tile_in{q}"], 16 * (m + 1))
                seen(pe, S["x_lo"], j)
                nc.tensor.transpose(post_ps[:, 0:P], x_in_tile[q][:, 0:C], ident[:, :]).then_inc(S["x_tile_T"], 1)

            def tile_up(j, q, e, half):
                dst, o = (g_ps[q % 2], 0) if half == 0 else (u_ps[q % 2], HID)
                return passes(dst, [xT_tile[q % 2][:, a, :] for a in range(2)],
                              [w[:, bass.ds(e, 1), o:o + HID].rearrange("p a n -> p (a n)") for w in (up_hi, up_lo)], True, True)

            def tile_g(m, q, e):
                j = RING * m + q
                seen(pe, S["x_lo"], j + 1)
                seen(pe, S["h_done"], j - 1)
                tile_up(j, q, e, 0).then_inc(S["g_ready"], 1)

            def tile_u(m, q, e):
                tile_up(2 * m + q, q, e, 1).then_inc(S["u_ready"], 1)

            def tile_hT(m, q):
                j = RING * m + q
                seen(pe, S["h_done"], j + 1)
                seen(pe, S["hT_copied"], j)
                for k in range(HC):
                    last = nc.tensor.transpose(out_ps[:, k * P:(k + 1) * P], h_sb[q % 2][:, k * P:(k + 1) * P], ident[:, :])
                last.then_inc(S["hT_ready"], 1)

            def tile_down(m, q, e):
                j = RING * m + q
                seen(pe, S["hT_copied"], j + 1)
                seen(pe, S["eo_done"], j - 1)
                for k in range(HC):
                    last = nc.tensor.matmul(eo_ps[q % 2], hT_sb[q % 2][:, k * P:(k + 1) * P],
                                            W_dn[:, bass.ds(e, 1), k, :].rearrange("p a c -> p (a c)"),
                                            start=(k == 0), stop=(k == HC - 1))
                last.then_inc(S["eo_ready"], 1)

            expert_reg = [nc.tensor.alloc_register(f"expert{q}") for q in range(RING)]

            def load_expert(m, q):
                nc.tensor.reg_load(expert_reg[q], table[0:1, 0, bass.ds(RING * m + q, 1)])

            def expert(q):
                return nc.tensor.snap(expert_reg[q], min_val=0, max_val=E - 1)

            def turn(m, q, first=False, last=False, drain=False):
                if not last and not drain:
                    tile_xT(*after(m, q))
                if not first:
                    tile_hT(*before(m, q))
                if not drain:
                    e = expert(q)
                    tile_g(m, q, e)
                if not drain:
                    tile_u(m, q, e)
                if not last and not drain:
                    load_expert(*after(m, q))
                if not first:
                    tile_down(*before(m, q), expert((q - 1) % RING))

            pe.wait_ge(S["table_done"], 1)
            pe.wait_ge(S["split_lo"], E)
            pe.wait_ge(S["ffn_down_in"], 16 * E)
            load_expert(0, 0)
            tile_xT(0, 0)
            for q in range(RING):
                turn(0, q, first=(q == 0))
            with pe.Fori(1, TURNS) as m:
                for q in range(RING):
                    turn(m, q)
            for q in range(LEFT):
                turn(TURNS, q, last=(q == LEFT - 1))
            turn(TURNS, LEFT, drain=True)


_INS = {"L0_attn_x": (NTOK, C), "L0_attn_w_kv_down": None, "L0_attn_w_kv_up": None, "L0_attn_w_q": None,
        "L0_attn_w_out": None, "L0_ffn_Wr": None, "L0_ffn_Wg": None, "L0_ffn_Wu": None, "L0_ffn_Wd": None}


def kernel(**inputs):
    import concourse.bacc as bacc
    from concourse.bass_utils import run_bass_kernel_spmd

    nc = bacc.Bacc("TRN2", target_bir_lowering=False, num_devices=1)
    arrays, args = {}, []
    for name, shape in _INS.items():
        a = np.ascontiguousarray(inputs[name])
        a = a.reshape(shape) if shape else a
        arrays[f"in_{name}"] = a
        args.append(nc.dram_tensor(f"in_{name}", a.shape, mybir.dt.from_np(a.dtype), kind="ExternalInput").ap())
    args.append(nc.dram_tensor("out_0", (NTOK, C), F32, kind="ExternalOutput").ap())
    layer(nc, *args)
    r = run_bass_kernel_spmd(nc, [arrays], core_ids=[0])
    return r.results[0]["out_0"].reshape(B, T, C)
```
